# Optimizing a Trainium2 kernel written in Bass

```python
import numpy as np
import jax
import jax.numpy as jnp

def _softmax(x, axis=-1):
    return jax.nn.softmax(x, axis=axis)

def _gelu(x):
    return jax.nn.gelu(x, approximate=True)

def _silu(x):
    return jax.nn.silu(x)

def _sigmoid(x):
    return jax.nn.sigmoid(x)

def _layernorm(x, axis=-1, eps=1e-05):
    m = jnp.mean(x, axis=axis, keepdims=True)
    v = jnp.var(x, axis=axis, keepdims=True)
    return (x - m) / jnp.sqrt(v + eps)

def _scatter_add(tgt, idx, src, axis=0):
    return tgt.at[idx].add(src)

def _segment_sum(src, seg, n):
    return jax.ops.segment_sum(src, seg, n)
kernel_name = 'mk_gps_d1_gnn_r8_fbaa57'

def setup_inputs(seed: int=0):
    np.random.seed(seed)
    _w = jnp.asarray

    def _rec_inputs():
        import jax
        import jax.numpy as jnp
        _gk = jax.random.key(seed)
        x = -0.0002117 + 1 * jax.random.normal(jax.random.fold_in(_gk, 1), (1250, 1024), jnp.float32)
        src = jax.random.randint(jax.random.fold_in(_gk, 2), (20000,), 0, 1250, jnp.int32)
        dst = jnp.minimum((1250 * jax.random.uniform(jax.random.fold_in(_gk, 3), (20000,)) ** 2.0).astype(jnp.int32), 9999)
        _o = jnp.argsort(dst, stable=True)
        src = src[_o]
        dst = dst[_o]
        return (x, src, dst)
    x, src, dst = _rec_inputs()

    def _L0_gnn_setup():
        import jax, jax.numpy as jnp
        import numpy as np
        N_NODES = 3125
        N_EDGES = 50000
        D = 1024

        def _sage_layer(h, edge_src, edge_dst, deg_inv, W_self, W_neigh, b):
            msg = h[edge_src]
            agg = jax.ops.segment_sum(msg, edge_dst, num_segments=h.shape[0])
            mean = agg * deg_inv[:, None]
            return h @ W_self + mean @ W_neigh + b
        key = jax.random.key(seed)
        ks = jax.random.split(key, 8)
        s = 1.0 / np.sqrt(D)
        return {'x': jax.random.normal(ks[0], (N_NODES, D), dtype=jnp.float32), 'edge_src': jax.random.randint(ks[1], (N_EDGES,), 0, N_NODES, dtype=jnp.int32), 'edge_dst': jax.random.randint(ks[2], (N_EDGES,), 0, N_NODES, dtype=jnp.int32), 'W_self0': jax.random.normal(ks[3], (D, D), dtype=jnp.float32) * s, 'W_neigh0': jax.random.normal(ks[4], (D, D), dtype=jnp.float32) * s, 'b0': jnp.zeros((D,), dtype=jnp.float32), 'W_self1': jax.random.normal(ks[5], (D, D), dtype=jnp.float32) * s, 'W_neigh1': jax.random.normal(ks[6], (D, D), dtype=jnp.float32) * s, 'b1': jnp.zeros((D,), dtype=jnp.float32)}
    _L0_gnn_all = _L0_gnn_setup()
    _L0_gnn_in = {k: v for k, v in _L0_gnn_all.items() if k in ('W_self0', 'W_neigh0', 'b0', 'W_self1', 'W_neigh1', 'b1')}
    del _L0_gnn_all

    def _L0_mix_setup():
        import jax, jax.numpy as jnp
        import numpy as np
        B, L, D = (2, 256, 1024)
        H = 16
        DH = D // H
        key = jax.random.key(seed)
        ks = jax.random.split(key, 9)
        s = 1.0 / np.sqrt(D)
        return {'x': jax.random.normal(ks[0], (B, L, D), dtype=jnp.float32), 'Wq': jax.random.normal(ks[1], (D, D), dtype=jnp.float32) * s, 'bq': jnp.zeros((D,), dtype=jnp.float32), 'Wk': jax.random.normal(ks[2], (D, D), dtype=jnp.float32) * s, 'bk': jnp.zeros((D,), dtype=jnp.float32), 'Wv': jax.random.normal(ks[3], (D, D), dtype=jnp.float32) * s, 'bv': jnp.zeros((D,), dtype=jnp.float32), 'Wo': jax.random.normal(ks[4], (D, D), dtype=jnp.float32) * s, 'bo': jnp.zeros((D,), dtype=jnp.float32)}
    _L0_mix_all = _L0_mix_setup()
    _L0_mix_in = {k: v for k, v in _L0_mix_all.items() if k in ('Wq', 'bq', 'Wk', 'bk', 'Wv', 'bv', 'Wo', 'bo')}
    del _L0_mix_all

    def _L0_ffn_setup():
        import jax, jax.numpy as jnp
        import numpy as np
        EMBED_DIM = 1024
        HIDDEN = 4 * EMBED_DIM
        BATCH, SEQ = (4, 512)
        EPS = 1e-05

        def _quant_weight(w):
            s = jnp.clip(jnp.mean(jnp.abs(w)), EPS, None)
            wq = jnp.clip(jnp.round(w / s), -1.0, 1.0) * s
            return w + jax.lax.stop_gradient(wq - w)

        def _quant_act(x):
            scale = 127.0 / jnp.clip(jnp.max(jnp.abs(x), axis=-1, keepdims=True), EPS, None)
            xq = jnp.clip(jnp.round(x * scale), -128.0, 127.0) / scale
            return x + jax.lax.stop_gradient(xq - x)

        def _bitlinear(x, w):
            return jnp.einsum('bsi,oi->bso', _quant_act(x), _quant_weight(w))
        key = jax.random.key(seed)
        k1, k2, k3 = jax.random.split(key, 3)
        x = jax.random.normal(k1, (BATCH, SEQ, EMBED_DIM), dtype=jnp.float32)
        w1 = jax.random.normal(k2, (HIDDEN, EMBED_DIM), dtype=jnp.float32) * (1.0 / np.sqrt(EMBED_DIM))
        w2 = jax.random.normal(k3, (EMBED_DIM, HIDDEN), dtype=jnp.float32) * (1.0 / np.sqrt(HIDDEN))
        return {'x': x, 'w1': w1, 'w2': w2}
    _L0_ffn_all = _L0_ffn_setup()
    _L0_ffn_in = {k: v for k, v in _L0_ffn_all.items() if k in ('w1', 'w2')}
    del _L0_ffn_all
    return {'x': x, 'src': src, 'dst': dst, 'L0_gnn_W_self0': _L0_gnn_in['W_self0'], 'L0_gnn_W_neigh0': _L0_gnn_in['W_neigh0'], 'L0_gnn_b0': _L0_gnn_in['b0'], 'L0_gnn_W_self1': _L0_gnn_in['W_self1'], 'L0_gnn_W_neigh1': _L0_gnn_in['W_neigh1'], 'L0_gnn_b1': _L0_gnn_in['b1'], 'L0_mix_Wq': _L0_mix_in['Wq'], 'L0_mix_bq': _L0_mix_in['bq'], 'L0_mix_Wk': _L0_mix_in['Wk'], 'L0_mix_bk': _L0_mix_in['bk'], 'L0_mix_Wv': _L0_mix_in['Wv'], 'L0_mix_bv': _L0_mix_in['bv'], 'L0_mix_Wo': _L0_mix_in['Wo'], 'L0_mix_bo': _L0_mix_in['bo'], 'L0_ffn_w1': _L0_ffn_in['w1'], 'L0_ffn_w2': _L0_ffn_in['w2']}

def reference(x, src, dst, L0_gnn_W_self0, L0_gnn_W_neigh0, L0_gnn_b0, L0_gnn_W_self1, L0_gnn_W_neigh1, L0_gnn_b1, L0_mix_Wq, L0_mix_bq, L0_mix_Wk, L0_mix_bk, L0_mix_Wv, L0_mix_bv, L0_mix_Wo, L0_mix_bo, L0_ffn_w1, L0_ffn_w2):
    import jax
    import jax.numpy as jnp

    def _L0_gnn_ref(x, edge_src, edge_dst, W_self0, W_neigh0, b0, W_self1, W_neigh1, b1):
        import jax, jax.numpy as jnp
        import numpy as np
        N_NODES = 3125
        N_EDGES = 50000
        D = 1024

        def _sage_layer(h, edge_src, edge_dst, deg_inv, W_self, W_neigh, b):
            msg = h[edge_src]
            agg = jax.ops.segment_sum(msg, edge_dst, num_segments=h.shape[0])
            mean = agg * deg_inv[:, None]
            return h @ W_self + mean @ W_neigh + b
        N = x.shape[0]
        deg = jax.ops.segment_sum(jnp.ones_like(edge_dst, dtype=x.dtype), edge_dst, num_segments=N)
        deg_inv = 1.0 / jnp.maximum(deg, 1.0)
        h = jax.nn.relu(_sage_layer(x, edge_src, edge_dst, deg_inv, W_self0, W_neigh0, b0))
        out = _sage_layer(h, edge_src, edge_dst, deg_inv, W_self1, W_neigh1, b1)
        return out

    def _L0_mix_ref(x, Wq, bq, Wk, bk, Wv, bv, Wo, bo):
        import jax, jax.numpy as jnp
        import numpy as np
        B, L, D = (2, 256, 1024)
        H = 16
        DH = D // H
        b, l, _ = x.shape

        def split_heads(t):
            return t.reshape(b, l, H, DH).transpose((0, 2, 1, 3))
        q = jax.nn.relu(split_heads(x @ Wq + bq))
        k = jax.nn.relu(split_heads(x @ Wk + bk))
        v = split_heads(x @ Wv + bv)
        context = jnp.einsum('bhld,bhkd->bhlk', q, k) / (l * DH)
        attn = jnp.einsum('bhlk,bhkd->bhld', context, v)
        attn = attn.transpose((0, 2, 1, 3)).reshape(b, l, D)
        return attn @ Wo + bo

    def _L0_ffn_ref(x, w1, w2):
        import jax, jax.numpy as jnp
        import numpy as np
        EMBED_DIM = 1024
        HIDDEN = 4 * EMBED_DIM
        BATCH, SEQ = (4, 512)
        EPS = 1e-05

        def _quant_weight(w):
            s = jnp.clip(jnp.mean(jnp.abs(w)), EPS, None)
            wq = jnp.clip(jnp.round(w / s), -1.0, 1.0) * s
            return w + jax.lax.stop_gradient(wq - w)

        def _quant_act(x):
            scale = 127.0 / jnp.clip(jnp.max(jnp.abs(x), axis=-1, keepdims=True), EPS, None)
            xq = jnp.clip(jnp.round(x * scale), -128.0, 127.0) / scale
            return x + jax.lax.stop_gradient(xq - x)

        def _bitlinear(x, w):
            return jnp.einsum('bsi,oi->bso', _quant_act(x), _quant_weight(w))
        h = jax.nn.gelu(_bitlinear(x, w1), approximate=False)
        return _bitlinear(h, w2)
    xn = _layernorm(x, axis=-1)
    x = x + _L0_gnn_ref(xn, src, dst, L0_gnn_W_self0, L0_gnn_W_neigh0, L0_gnn_b0, L0_gnn_W_self1, L0_gnn_W_neigh1, L0_gnn_b1) + _L0_mix_ref(xn[None], L0_mix_Wq, L0_mix_bq, L0_mix_Wk, L0_mix_bk, L0_mix_Wv, L0_mix_bv, L0_mix_Wo, L0_mix_bo)[0]
    x = x + _L0_ffn_ref(_layernorm(x, axis=-1)[None], L0_ffn_w1, L0_ffn_w2)[0]
    return x

_drawn_inputs = setup_inputs


def setup_inputs(seed=0):
    import zlib

    import numpy as np

    out = dict(_drawn_inputs(seed))
    spreads = {'L0_gnn_b0': (0.0, 0.8),
     'L0_gnn_b1': (0.0, 0.8),
     'L0_mix_bq': (0.0, 2.0),
     'L0_mix_bk': (0.0, 2.0),
     'L0_mix_bv': (0.0, 0.502),
     'L0_mix_bo': (0.0, 0.8)}
    factors = {'L0_mix_Wq': 8.0,
     'L0_mix_Wk': 8.0,
     'L0_mix_Wv': 7.895,
     'L0_mix_Wo': 3.684,
     'L0_gnn_W_neigh0': 5.583,
     'L0_ffn_w1': 4.824,
     'L0_ffn_w2': 4.534}
    for name, (base, spread) in spreads.items():
        noise = np.random.default_rng([zlib.crc32(name.encode()), seed]).standard_normal(out[name].shape)
        drawn = base * np.exp(spread * noise) if base else spread * noise
        out[name] = jnp.asarray(drawn.astype(out[name].dtype))
    for name, factor in factors.items():
        out[name] = (out[name] * factor).astype(out[name].dtype)
    return out
```

```python
from contextlib import ExitStack

import concourse.bass as bass
from concourse import mybir

F32, F16, F8, I32 = mybir.dt.float32, mybir.dt.float16, mybir.dt.float8e4, mybir.dt.int32
ACT = mybir.ActivationFunctionType
ALU = mybir.AluOpType
AXX = mybir.AxisListType.X
RMAX = bass.bass_isa.ReduceOp.max

P = 128
N = 1250
NT = -(-N // P)
NP_ = NT * P
D = 1024
KC = D // P
HID = 4 * D
HC = HID // P
DH = 64
NE = 20000
EC = -(-NE // P)
BANK = 512
RING = 8
EPS_LN, EPS_Q = 1e-5, 1e-5
MAGIC = 1.5 * 2.0 ** 23
TINY = 2.0 ** -60
POW2_MASK = 0x7F800000
X_SCALE = 2.0 ** 10
W_SCALE = 2.0 ** 14
XW = X_SCALE * W_SCALE
Z0_SCALE = 2.0 ** -15
MEANS = 8
WK, WV, WQ, WO, WN0, WS0, WN1, WS1 = range(8)
NORM_AT = {1: 6 * BANK, 2: 7 * BANK, 3: 2 * BANK, 4: 6 * BANK, 5: 6 * BANK}
MEAN_AT = 7 * BANK


def gps_kernel(nc, x, src_cols, dst_cols, dst_rows, Wself0, Wneigh0, b0, Wself1, Wneigh1, b1,
               Wq, bq_cols, Wk, bk, Wv, bv, Wo, bo, w1t, w2t, out):
    ctx = ExitStack()
    with ctx:
        def sb(name, shape, dt):
            return ctx.enter_context(nc.sbuf_tensor(name, shape, dt))

        named = {}

        def S(name):
            if name not in named:
                named[name] = ctx.enter_context(nc.semaphore(name))
            return named[name]

        XH = sb("XH", [P, 2, KC, NP_], F16)
        Zb = sb("Zb", [P, 2 * NT * D], F16)
        S0 = sb("S0", [P, 2 * KC * D], F16)
        S1 = sb("S1", [P, 2 * KC * D], F16)
        AT = sb("AT", [P, NT * NP_], F16)
        STREAM = sb("STREAM", [P, 4, D], F32)
        SPLIT = sb("SPLIT", [P, 2, D], F32)
        XIN = sb("XIN", [P, 2, D], F32)
        TMP = sb("TMP", [P, 2, D], F32)
        HL = sb("HL", [P, 2, 2, D], F16)
        ident = sb("ident", [P, P], F16)
        zero = sb("zero", [P, P], F16)
        ones = sb("ones", [P, P], F32)
        srcf = sb("srcf", [P, EC], F32)
        dstf = sb("dstf", [P, EC], F32)
        bnd = sb("bnd", [P, 2, NT], I32)
        NPW = sb("NPW", [P, 8, KC], F32)
        MW = sb("MW", [P, 2, HC], F32)
        st = sb("st", [P, 12], F32)
        mv = sb("mv", [P, 2], F32)
        AM = sb("AM", [P, 4], F32)
        widths = dict(
            magic=1, eps=1, first=NT, chunk1=2, chunk_left=2,
            ln_std=1, ln_rstd=1, p=8, s=8, sq0=1, sq1=1, norm_kv0=1, norm_kv1=1, a_kv0=1, a_kv1=1, c_kv0=1, c_kv1=1,
            sq6=7, norm6=7, bq=KC, bq2=KC, bqs=KC, a_q=1, c_q=1, kv_sq=1, norm_m=1, a_m=1, c_u=1, inv=1, tmp=1,
            w_sum=2, w_mean=2, thr=2, nthr=2, nsw=2, deg=NT, deg_h=NT, deg_x=NT, a_h=1, c_h=1, c_x=1,
            h_sq=NT, sq_h=1, norm_h=1, f_z1=1, y_std=1, y_rstd=1, y_max=1, y_clip=1, y_inv=1, y_sc=1, dq1=NT,
            g_max=1, g_clip=1, g_inv=1, g_sc=1, dq2=2)
        first_col, n_cols = {}, 0
        for name, n in widths.items():
            first_col[name] = n_cols
            n_cols += n
        cols = sb("cols", [P, n_cols], F32)

        def col(name):
            return cols[:, first_col[name]:first_col[name] + widths[name]]

        def at(name, i):
            return cols[:, bass.ds(i + first_col[name], 1)]

        ps = ctx.enter_context(nc.psum_tensor("ps", [P, 8 * BANK], F32))

        def banks(a, n=2, cut=None):
            return ps[:, a * BANK:a * BANK + (cut or n * BANK)]

        def turned(bank):
            return ps[:, bank * BANK:(bank + 1) * BANK].bitcast(F16).rearrange("p (k n) -> p k n", n=P)

        def weight(region):
            return region[:, 0:2 * KC * D].rearrange("p (k h n) -> p k h n", k=KC, h=2)

        Wk_s, Wv_s, Wq_s, M_s = weight(Zb), weight(S1), weight(S0), weight(S1)
        raw = S0[:, :].bitcast(F32).rearrange("p (k n) -> p k n", k=KC)
        Wo_raw = S1[:, :].bitcast(F32).rearrange("p (k n) -> p k n", k=KC)
        qT = Zb[:, :].rearrange("p (h k n) -> p h k n", h=2, k=KC)
        Z = Zb[:, :].rearrange("p (h t n) -> p h t n", h=2, t=NT)
        hot_src = Zb[:, 0:RING * NP_].rearrange("p (r n) -> p r n", r=RING)
        hot_dst = Zb[:, RING * NP_:RING * (NP_ + P)].rearrange("p (r n) -> p r n", r=RING)
        a_row = Zb[:, RING * (NP_ + P):RING * (NP_ + P) + 2 * NP_].rearrange("p (r n) -> p r n", r=2)
        iota = HL[:, :, :, :].rearrange("p a b n -> p (a b n)")[:, 0:NP_]
        kv = AT[:, 0:8 * D].rearrange("p (r q n) -> p r q n", r=2, q=4)
        b_kv = AT[:, 8 * D:12 * D].bitcast(F32).rearrange("p (a n) -> p a n", a=2)
        q_t = AT[:, 0:4 * NP_].bitcast(F32).rearrange("p (r n) -> p r n", r=2)
        edges = AT[:, 5 * D:5 * D + 4 * EC].bitcast(I32).rearrange("p (a c) -> p a c", a=2)
        d_int = AT[:, 6 * D:6 * D + 512].bitcast(I32).rearrange("p (g e) -> p g e", g=2)
        d_flt = AT[:, 6 * D + 512:7 * D].bitcast(F32).rearrange("p (g e) -> p g e", g=2)
        blk = AT[:, 7 * D:7 * D + 512].bitcast(F32)
        kvT = AT[:, 8 * D:10 * D].bitcast(F32)
        b_out = AT[:, 10 * D:12 * D].bitcast(F32)
        u_out = AT[:, 0:4 * D].bitcast(F32).rearrange("p (r n) -> p r n", r=2)
        ATv = AT[:, :].rearrange("p (s n) -> p s n", s=NT)
        x1_in = AT[:, 0:4 * D].bitcast(F32).rearrange("p (r n) -> p r n", r=2)
        y_out = AT[:, 4 * D:8 * D].bitcast(F32).rearrange("p (r n) -> p r n", r=2)
        w1q = S0[:, :].bitcast(F8)[:, 0:KC * HID].rearrange("p (k n) -> p k n", k=KC)
        w2q = S1[:, :].bitcast(F8)[:, 0:HC * D].rearrange("p (k n) -> p k n", k=HC)
        r_rows = HL[:, 0, :, :]
        x2n = HL[:, 1, :, :].rearrange("p a n -> p (a n)").bitcast(F32)
        hid = Zb[:, 0:4 * HID].bitcast(F32).rearrange("p (r n) -> p r n", r=2)
        hid_q = Zb[:, 4 * HID:5 * HID]
        hid_T = XH[:, 1, :, :].rearrange("p k n -> p (k n)")[:, 0:2 * HID].rearrange(
            "p (r k n) -> p r k n", r=2, k=HC)
        x2T = XH[:, 0, :, :]
        x2_tile = SPLIT[:, 1, :].bitcast(F16).rearrange("p (r k n) -> p r k n", r=2, k=KC)

        def ternary(region):
            v = region.bitcast(F8)
            return v[:, 0:2 * D].rearrange("p (r n) -> p r n", r=2), v[:, 2 * D:3 * D]

        q8_of = {0: ternary(XIN[:, 0, :]), 1: ternary(SPLIT[:, 0, :])}

        u_d = nc.dram_tensor("u_scratch", (NP_, D), F32, kind="Internal").ap()
        x1_d = nc.dram_tensor("x1_scratch", (NP_, D), F32, kind="Internal").ap()
        wq_d = [nc.dram_tensor(f"w{w + 1}q_scratch", (P, HC * D // 2), F16, kind="Internal").ap() for w in range(2)]

        def wait(eng, name, count):
            if not isinstance(count, int) or count > 0:
                eng.wait_ge(S(name), count)

        def alone(eng):
            eng.sem_inc(S("alone_" + eng.engine.name), 1)

        def rows(dram, t):
            return dram[bass.ds(t * P, P), :]

        def tile_of(t):
            return bass.ds(t * P, P)

        streamed = {WQ: Wq, WO: Wo, WN0: Wneigh0, WS0: Wself0, WN1: Wneigh1, WS1: Wself1}
        w1_chunk = w1t.rearrange("(k p) (q n) -> p k q n", p=P, n=D)

        def quant_src(w, i, j):
            if w == 0:
                return w1t[bass.ds(i * P, P), j * D:(j + 1) * D]
            return w2t[bass.ds(i * 4 * P + j * P, P), :]

        def steps(eng, a, b, body):
            assert (b - a) % 2 == 0
            with eng.Fori(0, (b - a) // 2) as pair:
                for j in range(2):
                    body(pair * 2 + (a + j), j)

        block = ctx.enter_context(nc.Block())

        @block.sync
        def _(sp):
            def load_x(t, slot):
                sp.dma_start(XIN[:, slot, :], rows(x, t)).then_inc(S(f"x_in{slot}"), 16)

            def load_split(dram, kc, slot, idx):
                sp.wait_ge(S("split_lo"), idx - 1)
                sp.dma_start(SPLIT[:, slot, :], rows(dram, kc)).then_inc(S(f"split_in{slot}"), 16)

            load_x(0, 0)
            for kc in range(KC):
                sp.dma_start(raw[:, kc, :], Wk[kc * P:(kc + 1) * P, :]).then_inc(S(f"raw_in{kc}"), 16)
            sp.dma_start(b_kv[:, 0, :], bk.partition_broadcast(P)).then_inc(S("bk_in"), 16)
            sp.dma_start(b_kv[:, 1, :], bv.partition_broadcast(P)).then_inc(S("bv_in"), 16)
            load_x(1, 1)
            for kc in range(KC):
                sp.wait_ge(S("split_lo"), kc + 1)
                sp.dma_start(raw[:, kc, :], Wv[kc * P:(kc + 1) * P, :]).then_inc(S(f"raw_in{kc}"), 16)
            sp.dma_start(col("bq"), bq_cols).then_inc(S("bq_in"), 16)

            def kv_loads(t, j):
                sp.wait_ge(S("ln_xn"), t)
                load_x(t + 1, j)
                for n, w in enumerate((WQ, WO, WN0, WS0, WN1, WS1)):
                    slot = (6 * j + n) % 4
                    i = 6 * (t - 1) + n
                    wait(sp, "stream_used", i - 3)
                    sp.dma_start(STREAM[:, slot, :], rows(streamed[w], t - 1)).then_inc(S(f"stream_in{slot}"), 16)

            kv_loads(1, 0)
            kv_loads(2, 1)
            steps(sp, 3, 9, kv_loads)
            for kc in range(KC):
                load_split(Wq, kc, kc % 2, 16 + kc)

            sp.wait_ge(S("v_ps"), NT)
            sp.dma_start(Wo_raw, Wo.rearrange("(k p) n -> p k n", p=P)).then_inc(S("wo_in"), 16)
            sp.wait_ge(S("v_t"), NT)
            sp.wait_ge(S("kv_ps"), NT)
            sp.dma_start(edges[:, 0, :], src_cols).then_inc(S("src_in"), 16)
            sp.dma_start(edges[:, 1, :], dst_cols).then_inc(S("dst_in"), 16)
            sp.dma_start(d_int, dst_rows.rearrange("(g p) e -> p g e", p=P)).then_inc(S("rows_in"), 16)
            sp.dma_start(b_out, b1.partition_broadcast(P)).then_inc(S("b1_in"), 16)
            sp.dma_start(TMP[:, 1, :], bo.partition_broadcast(P)).then_inc(S("bo_in"), 16)
            for w in range(2):
                with sp.Fori(0, 8) as i:
                    for j in range(4):
                        c = 48 + 32 * w + 4 * i + j
                        sp.wait_ge(S("stream_used"), c - 3)
                        sp.dma_start(STREAM[:, j, :], quant_src(w, i, j))\
                            .then_inc(S(f"stream_in{j}"), 16)

            sp.wait_ge(S("ln_xn"), NT)
            load_x(0, 0)
            load_x(1, 1)

            def u_moves(t, j, split=True):
                if split:
                    load_split(Wneigh0, t, j, 24 + t)
                sp.wait_ge(S("u"), t + 1)
                sp.dma_start(rows(u_d, t), u_out[:, j, :]).then_inc(S(f"u_out{j}"), 16)
                if split:
                    load_x(t + 2, j)

            steps(sp, 0, 8, u_moves)
            for t in range(8, NT):
                u_moves(t, t % 2, False)
            sp.dma_start(XIN[:, 1, :], b0.partition_broadcast(P)).then_inc(S("b0_in"), 16)

            sp.wait_ge(S("u_ps"), NT)
            steps(sp, 0, 8, lambda t, j: load_split(Wself0, t, j, 32 + t))

            def quant_moves(w, t, j, more=True):
                for n in range(4):
                    c = 32 * w + 4 * t + n
                    sp.wait_ge(S("quantized"), c + 1)
                    sp.dma_start(wq_d[w][:, bass.ds((4 * t + n) * (D // 2), D // 2)],
                                 q8_of[w][0][:, n % 2, :].bitcast(F16))\
                        .then_inc(S(f"q8_out{n % 2}"), 16)
                    if more:
                        sp.dma_start(STREAM[:, n, :], quant_src(w, t + 1, n)).then_inc(S(f"stream_in{n}"), 16)

            sp.wait_ge(S("stream_used"), 112)
            for n in range(4):
                sp.dma_start(STREAM[:, n, :], quant_src(0, 0, n)).then_inc(S(f"stream_in{n}"), 16)

            def h_moves(t, j, more=True):
                load_split(Wneigh1, t, j, 40 + t)
                quant_moves(0, t, j, more)

            steps(sp, 0, 6, h_moves)
            h_moves(6, 0)
            h_moves(7, 1, False)

            for t in range(2):
                sp.wait_ge(S(f"u_out{t}"), 16 * NT // 2)
                if t == 1:
                    sp.wait_ge(S("h_t1"), NT)
                else:
                    sp.wait_ge(S("q8_out0"), 16 * 16)
                    sp.wait_ge(S("q8_out1"), 16 * 16)
                sp.dma_start(XIN[:, t, :], rows(u_d, t)).then_inc(S(f"x_in{t}"), 16)
            steps(sp, 0, 8, lambda t, j: load_split(Wself1, t, j, 48 + t))
            sp.wait_ge(S("quantized"), 32)
            for n in range(4):
                sp.dma_start(STREAM[:, n, :], quant_src(1, 0, n)).then_inc(S(f"stream_in{n}"), 16)

            sp.wait_ge(S("z1_ps"), NT)
            sp.dma_start(S0[:, :], wq_d[0]).then_inc(S("w1q_in"), 16)
            sp.wait_ge(S("split_lo"), 56)

            def x1_moves(t, j, quant=True, more=True):
                if quant:
                    quant_moves(1, t, j, more)
                    sp.wait_ge(S("x1_t1"), t + 1)
                    sp.dma_start(XIN[:, j, :], rows(u_d, t + 2)).then_inc(S(f"x_in{j}"), 16)
                sp.wait_ge(S("x1"), t + 1)
                sp.dma_start(rows(x1_d, t), TMP[:, 1, :]).then_inc(S("x1_out"), 16)

            steps(sp, 0, 6, x1_moves)
            x1_moves(6, 0)
            x1_moves(7, 1, True, False)
            x1_moves(8, 0, False)
            x1_moves(9, 1, False)

            sp.wait_ge(S("s1_ps"), NT)
            sp.wait_ge(S("q8_out0"), 32 * 16)
            sp.wait_ge(S("q8_out1"), 32 * 16)
            sp.dma_start(S1[:, :], wq_d[1]).then_inc(S("w2q_in"), 16)
            sp.wait_ge(S("x1_out"), 16 * NT)
            for t in range(2):
                sp.dma_start(x1_in[:, t, :], rows(x1_d, t)).then_inc(S(f"x1_in{t}"), 16)

            def y_moves(t, j, more=True):
                sp.wait_ge(S("y"), t + 1)
                sp.dma_start(rows(out, t), y_out[:, j, :]).then_inc(S(f"y_out{j}"), 16)
                if more:
                    sp.dma_start(x1_in[:, j, :], rows(x1_d, t + 2)).then_inc(S(f"x1_in{j}"), 16)

            steps(sp, 0, 8, y_moves)
            for t in range(8, NT):
                y_moves(t, t % 2, False)
            for j in range(2):
                sp.wait_ge(S(f"y_out{j}"), 16 * NT // 2)

        @block.gpsimd
        def _(pool):
            nc.gpsimd.memset(ident[:, :], 0.0).then_inc(S("ident0"), 1)
            pool.wait_ge(S("ident0"), 1)
            nc.gpsimd.affine_select(out=ident[:, :], in_=ident[:, :], compare_op=ALU.not_equal, fill=1.0, base=0,
                                    pattern=[[-1, P]], channel_multiplier=1).then_inc(S("ident"), 1)
            nc.gpsimd.memset(zero[:, :], 0.0).then_inc(S("zero"), 1)
            nc.gpsimd.memset(ones[:, :], 1.0).then_inc(S("ones"), 1)
            nc.gpsimd.memset(col("magic"), MAGIC).then_inc(S("consts"), 1)
            nc.gpsimd.memset(col("eps"), EPS_LN).then_inc(S("consts"), 1)
            nc.gpsimd.iota(col("first"), [[P, NT]], base=0, channel_multiplier=0,
                           allow_small_or_imprecise_dtypes=True).then_inc(S("consts"), 1)
            nc.gpsimd.iota(col("chunk1"), [[P, 2]], base=1, channel_multiplier=1,
                           allow_small_or_imprecise_dtypes=True).then_inc(S("consts"), 1)
            nc.gpsimd.iota(col("chunk_left"), [[-P, 2]], base=2 * P, channel_multiplier=-1,
                           allow_small_or_imprecise_dtypes=True).then_inc(S("consts"), 1)
            pool.wait_ge(S("v_t"), NT)
            nc.gpsimd.memset(kvT, 0.0).then_inc(S("kvT0"), 1)
            pool.wait_ge(S("blk_v"), 4)
            nc.gpsimd.partition_all_reduce(blk[:, 80:120], blk[:, 40:80], P, RMAX).then_inc(S("blk_r"), 1)
            pool.wait_ge(S("xT_lo"), NT)
            nc.gpsimd.iota(iota, [[1, NP_]], base=0, channel_multiplier=0,
                           allow_small_or_imprecise_dtypes=True).then_inc(S("iota"), 1)

            def x2_pool(t, j):
                pool.wait_ge(S("x2T"), t + 1)
                wait(pool, "f1_ps", 8 * (t - 1))
                nc.gpsimd.tensor_copy(x2_tile[:, j, :, :], x2T[:, :, tile_of(t)]).then_inc(S("x2_tile"), 1)

            pool.wait_ge(S("split_lo"), 56)
            x2_pool(0, 0)
            x2_pool(1, 1)
            steps(pool, 2, NT, x2_pool)

        @block.scalar
        def _(act):
            A = nc.scalar.activation

            def ln_act(t, j):
                act.wait_ge(S("ln_mv"), t + 1)
                A(col("ln_std"), mv[:, 1:2], ACT.Sqrt, bias=col("eps")).then_inc(S("ln_std"), 1)
                act.wait_ge(S("ln_xn"), t + 1)
                A(HL[:, j, 0, :], TMP[:, 0, :], ACT.Copy, scale=X_SCALE).then_inc(S("ln_hi"), 1)

            def xT_act(t):
                act.wait_ge(S("xT_ps"), 2 * t + 1)
                alone(act)
                A(XH[:, 0, :, tile_of(t)], turned(2), ACT.Copy).then_inc(S("xT_hi"), 1)

            def norm(name, n, count):
                act.wait_ge(S("norm_ps"), count)
                A(col(name), ps[:, NORM_AT[count]:NORM_AT[count] + n], ACT.Sqrt).then_inc(S("norm"), 1)

            def split(dst, src, scale):
                A(dst, src, ACT.Copy, scale=scale).then_inc(S("split_hi"), 1)

            def split_chunk(dst, kc, slot, idx, scale):
                act.wait_ge(S(f"split_in{slot}"), 8 * (idx - 16 - slot) + 16)
                alone(act)
                split(dst[:, kc, 0, :], SPLIT[:, slot, :], scale)

            act.wait_ge(S("consts"), 5)
            ln_act(0, 0)
            xT_act(0)
            for n, (w, dst) in enumerate(((WK, Wk_s), (WV, Wv_s))):
                for kc in range(KC):
                    act.wait_ge(S(f"raw_in{kc}"), 16 * (n + 1))
                    wait(act, "squared", 8 * n + kc - 3)
                    A(kv[:, 1, kc % 4, :], raw[:, kc, :], ACT.Square,
                      accum_out=NPW[:, w, kc:kc + 1]).then_inc(S("squared"), 1)
                norm("norm_kv" + str(n), 1, n + 1)
                act.wait_ge(S("scales"), n + 1)
                for kc in range(KC):
                    split(dst[:, kc, 0, :], raw[:, kc, :], at("s", w))
                if n == 0:
                    ln_act(1, 1)

            def kv_act(t, j, ln=True, norms=True):
                if ln:
                    if not (isinstance(t, int) and t == 0):
                        ln_act(t + 1, 1 - j)
                    xT_act(t + 1)
                act.wait_ge(S("k_t"), t + 1)
                A(kv[:, j, 0, :], TMP[:, 1, :], ACT.Relu).then_inc(S("k_hi"), 1)
                if norms:
                    for n, w in enumerate((WQ, WO, WN0, WS0, WN1, WS1)):
                        i = 6 * (1 - j) + n
                        act.wait_ge(S(f"stream_in{i % 4}"), 24 * (t - (2 - j)) + 16 * (i // 4) + 16)
                        alone(act)
                        A(STREAM[:, i % 4, :], STREAM[:, i % 4, :], ACT.Square,
                          accum_out=NPW[:, w, bass.ds(t - 1, 1)]).then_inc(S("stream_used"), 1)
                act.wait_ge(S("v_t"), t + 1)
                A(kv[:, j, 2, :], TMP[:, 1, :], ACT.Copy).then_inc(S("v_hi"), 1)

            kv_act(0, 0, norms=False)
            steps(act, 1, 9, lambda t, j: kv_act(t, 1 - j))
            norm("norm6", 7, 3)
            act.wait_ge(S("scales"), 3)
            for kc in range(KC):
                split_chunk(Wq_s, kc, kc % 2, 16 + kc, at("s", WQ))
            kv_act(9, 1, ln=False, norms=False)

            def q_act(m, j, w):
                act.wait_ge(S("q_t"), m + 1)
                alone(act)
                A(qT[:, 0, m, :], q_t[:, j, :], ACT.Relu).then_inc(S("q_hi"), 1)
                for n in range(MEANS):
                    act.wait_ge(S(f"stream_in{n % 4}"), 12 * 16 + 32 * m + 16 * (n // 4) + 16)
                    alone(act)
                    A(STREAM[:, n % 4, :], STREAM[:, n % 4, :], ACT.Abs,
                      accum_out=MW[:, w, bass.ds(8 * (m - 4 * w) + n, 1)]).then_inc(S("stream_used"), 1)

            act.wait_ge(S("c_q"), 1)
            act.wait_ge(S("kvT"), 16)
            A(banks(6), kvT, ACT.Square, accum_out=col("kv_sq")).then_inc(S("kv_sq"), 1)
            steps(act, 0, 4, lambda m, j: q_act(m, j, 0))
            steps(act, 4, 8, lambda m, j: q_act(m, j, 1))
            norm("norm_m", 1, 4)
            act.wait_ge(S("a_m"), 1)
            for p in range(KC):
                act.wait_ge(S("m_ps"), p + 1)
                A(M_s[:, p, 0, :], banks(2 * (p % 3)), ACT.Copy, scale=col("a_m")).then_inc(S("m_hi"), 1)

            steps(act, 0, 8, lambda t, j: split_chunk(weight(S0), t, j, 24 + t, at("s", WN0)))

            def aT_act(b):
                act.wait_ge(S("aT_ps"), 2 * b + 1)
                A(ATv[:, 0:8, b * P:(b + 1) * P], turned(6), ACT.Copy).then_inc(S("aT_hi"), 1)
                act.wait_ge(S("aT_ps"), 2 * b + 2)
                A(ATv[:, 8:NT, b * P:(b + 1) * P], turned(7)[:, 0:NT - 8, :], ACT.Copy).then_inc(S("aT_lo"), 1)

            for j in range(2):
                act.wait_ge(S(f"u_out{j}"), 16 * NT // 2)
            for b in range(NT):
                act.wait_ge(S("a_ps"), b + 1)
                A(a_row[:, b % 2, :], banks(3 * (b % 2), cut=NP_), ACT.Copy, accum_out=at("deg", b)).then_inc(S("a_row"), 1)
                if b >= 1:
                    aT_act(b - 1)
            aT_act(NT - 1)

            def z_act(name, t, j, scale):
                act.wait_ge(S(name + "_ps"), t + 1)
                alone(act)
                A(Z[:, 0, t, :], banks(2 * j), ACT.Copy, scale=scale).then_inc(S(name + "_hi"), 1)

            act.wait_ge(S("u_ps"), NT)

            def z0_act(t, j):
                split_chunk(weight(S1), t, j, 32 + t, at("s", WS0))
                z_act("z0", t, j, Z0_SCALE)

            steps(act, 0, 8, z0_act)
            for t in range(8, NT):
                z_act("z0", t, t % 2, Z0_SCALE)

            def hT_act(t):
                act.wait_ge(S("hT_ps"), 2 * t + 1)
                alone(act)
                A(XH[:, 0, :, tile_of(t)], turned(6), ACT.Copy).then_inc(S("hT_hi"), 1)

            def h_act(t, j, split_too=True, turn=True):
                if split_too:
                    split_chunk(weight(S0), t, j, 40 + t, at("s", WN1))
                if turn:
                    hT_act(t - 1)
                act.wait_ge(S("h_t2"), t + 1)
                A(HL[:, j, 0, :], TMP[:, 1, :], ACT.Relu).then_inc(S("h_hi"), 1)
                wait(act, "h_sq", t)
                act.wait_ge(S("h_hi"), t + 1)
                alone(act)
                A(banks(4), HL[:, j, 0, :], ACT.Square, accum_out=at("h_sq", t)).then_inc(S("h_sq"), 1)

            h_act(0, 0, turn=False)
            h_act(1, 1)
            steps(act, 2, 8, h_act)
            h_act(8, 0, False)
            h_act(9, 1, False)
            hT_act(9)

            norm("norm_h", 1, 5)
            act.wait_ge(S("f_z1"), 1)

            def z1_act(t, j):
                split_chunk(weight(S1), t, j, 48 + t, at("s", WS1))
                z_act("z1", t, j, col("f_z1"))

            steps(act, 0, 8, z1_act)
            for t in range(8, NT):
                z_act("z1", t, t % 2, col("f_z1"))

            def x1_act(t, j):
                act.wait_ge(S("y_mv"), t + 1)
                A(col("y_std"), mv[:, 1:2], ACT.Sqrt, bias=col("eps")).then_inc(S("y_std"), 1)
                act.wait_ge(S("y_sc"), t + 1)
                A(x2n, x2n, ACT.Identity, bias=col("magic"), scale=col("y_sc")).then_inc(S("r_magic"), 1)

            steps(act, 0, NT, x1_act)

            def gelu(t, slot):
                for n in range(8):
                    act.wait_ge(S("f1_ps"), 8 * t + n + 1)
                    alone(act)
                    A(hid[:, slot, n * BANK:(n + 1) * BANK], banks(n % 4, 1), ACT.Gelu,
                      scale=at("dq1", t)).then_inc(S("gelu"), 1)

            def hid_round(t, slot):
                act.wait_ge(S("g_sc"), t + 1)
                for n in range(4):
                    piece = hid[:, slot, n * D:(n + 1) * D]
                    A(piece, piece, ACT.Identity, bias=col("magic"), scale=col("g_sc")).then_inc(S("g_magic"), 1)

            def hidT_act(t, slot):
                for n in (0, 2):
                    act.wait_ge(S("gT_ps"), 4 * t + n + 1)
                    A(hid_T[:, slot, 8 * n:8 * n + 8, :], turned(6), ACT.Copy).then_inc(S("gT_hi"), 1)

            def ffn_act(t, j, more=True):
                hid_round(t, j)
                if more:
                    gelu(t + 1, 1 - j)
                hidT_act(t, j)

            gelu(0, 0)
            steps(act, 0, 8, ffn_act)
            ffn_act(8, 0)
            ffn_act(9, 1, False)

        @block.vector
        def _(dve):
            V = nc.vector
            small = [0]

            def link(ins):
                small[0] += 1
                ins.then_inc(S("cols"), 1)
                dve.wait_ge(S("cols"), small[0])

            def pow2(dst, a):
                link(V.tensor_scalar(dst, a, TINY, None, ALU.max))
                link(V.tensor_scalar(dst.bitcast(I32), dst.bitcast(I32), POW2_MASK, None, ALU.bitwise_and))

            def ratio(dst, a, num):
                link(V.reciprocal(dst, a))
                link(V.tensor_scalar(dst, dst, num, None, ALU.mult))

            def times(dst, a, b, c=1.0):
                link(V.tensor_scalar(dst, a, b, c, ALU.mult, ALU.mult))

            def range_scale(dst, a):
                pow2(dst, a)
                ratio(dst, dst, W_SCALE)

            def ln_dve(t, j):
                dve.wait_ge(S(f"x_in{j}"), 8 * (t - j) + 16)
                wait(dve, "ln_lo", t)
                for n in range(2):
                    V.bn_stats(st[:, 6 * n:6 * n + 6], XIN[:, j, n * 512:(n + 1) * 512]).then_inc(S("ln_stats"), 1)
                dve.wait_ge(S("ln_stats"), 2 * t + 2)
                alone(dve)
                V.bn_aggr(mv[:, :], st[:, :]).then_inc(S("ln_mv"), 1)
                dve.wait_ge(S("ln_std"), t + 1)
                V.reciprocal(col("ln_rstd"), col("ln_std")).then_inc(S("ln_rstd"), 1)
                dve.wait_ge(S("ln_rstd"), t + 1)
                V.tensor_scalar(TMP[:, 0, :], XIN[:, j, :], mv[:, 0:1], col("ln_rstd"),
                                ALU.subtract, ALU.mult).then_inc(S("ln_xn"), 1)
                dve.wait_ge(S("ln_hi"), t + 1)
                V.scalar_tensor_tensor(HL[:, j, 1, :], TMP[:, 0, :], X_SCALE, HL[:, j, 0, :],
                                       ALU.mult, ALU.subtract).then_inc(S("ln_lo"), 1)

            def xT_dve(t):
                dve.wait_ge(S("xT_ps"), 2 * t + 2)
                V.tensor_copy(XH[:, 1, :, tile_of(t)], turned(3)).then_inc(S("xT_lo"), 1)

            def split(dst, src, scale, idx):
                dve.wait_ge(S("split_hi"), idx + 1)
                V.scalar_tensor_tensor(dst[:, 1, :], src, scale, dst[:, 0, :],
                                       ALU.mult, ALU.subtract).then_inc(S("split_lo"), 1)

            def split_chunk(dst, kc, slot, idx, scale):
                dve.wait_ge(S("split_hi"), idx + 1)
                V.scalar_tensor_tensor(dst[:, kc, 1, :], SPLIT[:, slot, :], scale, dst[:, kc, 0, :],
                                       ALU.mult, ALU.subtract).then_inc(S("split_lo"), 1)

            dve.wait_ge(S("consts"), 5)
            ln_dve(0, 0)
            xT_dve(0)
            for n, (w, dst) in enumerate(((WK, Wk_s), (WV, Wv_s))):
                dve.wait_ge(S("squared"), 8 * (n + 1))
                V.tensor_reduce(col("sq" + str(n)), NPW[:, w, :], AXX, ALU.add).then_inc(S("sq"), 1)
                dve.wait_ge(S("norm"), n + 1)
                pow2(at("p", w), col("norm_kv" + str(n)))
                link(V.reciprocal(at("s", w), at("p", w)))
                V.tensor_scalar(at("s", w), at("s", w), W_SCALE, None, ALU.mult).then_inc(S("scales"), 1)
                dve.wait_ge(S("scales"), n + 1)
                a, c = col("a_kv" + str(n)), col("c_kv" + str(n))
                dve.wait_ge(S("bk_in" if n == 0 else "bv_in"), 16)
                link(V.tensor_reduce(a, b_kv[:, n, :], AXX, ALU.max, apply_absolute_value=True))
                link(V.scalar_tensor_tensor(a, at("p", w), 2.0 ** 6, a, ALU.mult, ALU.add))
                range_scale(a, a)
                link(V.tensor_scalar(b_kv[:, n, :], b_kv[:, n, :], a, None, ALU.mult))
                times(c, at("p", w), a, 1.0 / XW)
                for kc in range(KC):
                    split(dst[:, kc, :, :], raw[:, kc, :], at("s", w), 8 * n + kc)
                if n == 0:
                    ln_dve(1, 1)

            def kv_dve(t, j, ln=True):
                if ln:
                    if not (isinstance(t, int) and t == 0):
                        ln_dve(t + 1, 1 - j)
                    xT_dve(t + 1)
                for n, what in enumerate("kv"):
                    dve.wait_ge(S(what + "_ps"), t + 1)
                    if n == 0:
                        wait(dve, "v_lo", t)
                    else:
                        dve.wait_ge(S("k_lo"), t + 1)
                    V.scalar_tensor_tensor(TMP[:, 1, :], banks(4 * n), col("c_kv" + str(n)), b_kv[:, n, :],
                                           ALU.mult, ALU.add).then_inc(S(what + "_t"), 1)
                    dve.wait_ge(S(what + "_hi"), t + 1)
                    if n == 0:
                        V.scalar_tensor_tensor(kv[:, j, 1, :], TMP[:, 1, :], 0.0, kv[:, j, 0, :],
                                               ALU.max, ALU.subtract).then_inc(S("k_lo"), 1)
                    else:
                        V.tensor_tensor(kv[:, j, 3, :], TMP[:, 1, :], kv[:, j, 2, :],
                                        ALU.subtract).then_inc(S("v_lo"), 1)

            kv_dve(0, 0)
            steps(dve, 1, 9, lambda t, j: kv_dve(t, 1 - j))
            dve.wait_ge(S("stream_used"), 48)
            V.tensor_reduce(col("sq6")[:, 0:6], NPW[:, WQ:, :], AXX, ALU.add).then_inc(S("sq"), 1)
            dve.wait_ge(S("bq_in"), 16)
            link(V.tensor_tensor(col("bq2"), col("bq"), col("bq"), ALU.mult))
            V.tensor_reduce(col("sq6")[:, 6:7], col("bq2"), AXX, ALU.add).then_inc(S("sq"), 1)
            dve.wait_ge(S("norm"), 3)
            pw, sw = col("p")[:, WQ:], col("s")[:, WQ:]
            pow2(pw, col("norm6")[:, 0:6])
            link(V.reciprocal(sw, pw))
            V.tensor_scalar(sw, sw, W_SCALE, None, ALU.mult).then_inc(S("scales"), 1)
            dve.wait_ge(S("scales"), 3)
            for kc in range(KC):
                split_chunk(Wq_s, kc, kc % 2, 16 + kc, at("s", WQ))
            kv_dve(9, 1, ln=False)

            link(V.scalar_tensor_tensor(col("a_q"), at("p", WQ), 2.0 ** 6, col("norm6")[:, 6:7],
                                        ALU.mult, ALU.add))
            range_scale(col("a_q"), col("a_q"))
            times(col("c_q"), at("p", WQ), col("a_q"), 1.0 / XW)
            V.tensor_scalar(col("bqs"), col("bq"), col("a_q"), None, ALU.mult).then_inc(S("c_q"), 1)
            dve.wait_ge(S("c_q"), 1)
            dve.wait_ge(S("kv_ps"), NT)
            dve.wait_ge(S("kvT0"), 1)
            for p in range(KC):
                for h in range(2):
                    r = slice(DH * h, DH * h + DH)
                    c = P * p + DH * h
                    V.tensor_copy(kvT[r, c:c + DH], ps[r, 6 * BANK + c:6 * BANK + c + DH]).then_inc(S("kvT"), 1)

            dve.wait_ge(S("src_in"), 16)
            dve.wait_ge(S("dst_in"), 16)
            V.tensor_copy(srcf[:, :], edges[:, 0, :]).then_inc(S("edges_f"), 1)
            V.tensor_copy(dstf[:, :], edges[:, 1, :]).then_inc(S("edges_f"), 1)
            dve.wait_ge(S("rows_in"), 16)
            link(V.tensor_copy(d_flt, d_int))
            link(V.tensor_reduce(blk[:, 0:2], d_flt, AXX, ALU.min))
            link(V.tensor_reduce(blk[:, 2:4], d_flt, AXX, ALU.max))
            link(V.tensor_scalar(blk[:, 0:2], blk[:, 0:2], -(P - 1.0), None, ALU.add))
            for g in range(2):
                a, b = blk[:, 10:20], blk[:, 20:30]
                link(V.tensor_scalar(a, col("first"), blk[:, 2 + g:3 + g], None, ALU.is_le))
                link(V.tensor_scalar(b, col("first"), blk[:, g:g + 1], None, ALU.is_ge))
                link(V.tensor_tensor(a, a, b, ALU.mult))
                V.tensor_scalar(blk[:, 40 + 10 * g:50 + 10 * g], a, col("chunk_left")[:, g:g + 1], None,
                                ALU.mult).then_inc(S("blk_v"), 1)
                V.tensor_scalar(blk[:, 60 + 10 * g:70 + 10 * g], a, col("chunk1")[:, g:g + 1], None,
                                ALU.mult).then_inc(S("blk_v"), 1)
                dve.wait_ge(S("blk_v"), 2 * g + 2)
            dve.wait_ge(S("blk_r"), 1)
            lo, hi = blk[:, 0:10], blk[:, 10:20]
            link(V.tensor_tensor(lo, blk[:, 80:90], blk[:, 90:100], ALU.max))
            link(V.tensor_scalar(lo, lo, -1.0, 2.0 * P, ALU.mult, ALU.add))
            link(V.tensor_scalar(lo, lo, EC - 1.0, None, ALU.min))
            link(V.tensor_tensor(hi, blk[:, 100:110], blk[:, 110:120], ALU.max))
            link(V.tensor_scalar(blk[:, 20:30], lo, 1.0, None, ALU.add))
            link(V.tensor_tensor(hi, hi, blk[:, 20:30], ALU.max))
            V.tensor_copy(bnd[:, 0, :], lo).then_inc(S("bounds"), 1)
            V.tensor_copy(bnd[:, 1, :], hi).then_inc(S("bounds"), 1)

            def q_dve(m, j):
                dve.wait_ge(S("q_ps"), m + 1)
                wait(dve, "q_lo", m - 1)
                V.tensor_scalar(q_t[:, j, :], banks(3 * j, cut=NP_), col("c_q"), at("bqs", m),
                                ALU.mult, ALU.add).then_inc(S("q_t"), 1)
                dve.wait_ge(S("q_hi"), m + 1)
                V.scalar_tensor_tensor(qT[:, 1, m, :], q_t[:, j, :], 0.0, qT[:, 0, m, :],
                                       ALU.max, ALU.subtract).then_inc(S("q_lo"), 1)

            q_dve(0, 0)
            q_dve(1, 1)
            steps(dve, 2, 8, q_dve)

            dve.wait_ge(S("stream_used"), 112)
            dve.wait_ge(S("kv_sq"), 1)
            V.tensor_reduce(col("w_sum"), MW[:, :, :], AXX, ALU.add).then_inc(S("sq"), 1)
            dve.wait_ge(S("norm"), 4)
            times(col("a_m"), col("norm_m"), col("norm6")[:, 1:2])
            pow2(col("a_m"), col("a_m"))
            link(V.reciprocal(col("a_m"), col("a_m")))
            V.tensor_scalar(col("a_m"), col("a_m"), W_SCALE, None, ALU.mult).then_inc(S("a_m"), 1)
            dve.wait_ge(S("a_m"), 1)
            for p in range(KC):
                dve.wait_ge(S("m_hi"), p + 1)
                V.scalar_tensor_tensor(M_s[:, p, 1, :], banks(2 * (p % 3)), col("a_m"), M_s[:, p, 0, :],
                                       ALU.mult, ALU.subtract).then_inc(S("m_lo"), 1)
            dve.wait_ge(S("mean_ps"), 1)
            sw = col("w_mean")
            link(V.tensor_scalar(sw, ps[:, MEAN_AT:MEAN_AT + 2], 1.0 / (HID * D), EPS_Q, ALU.mult, ALU.max))
            link(V.tensor_scalar(col("thr"), sw, 0.5, None, ALU.mult))
            link(V.tensor_scalar(col("nthr"), sw, -0.5, None, ALU.mult))
            link(V.tensor_scalar(col("nsw"), sw, -1.0 / 127.0, None, ALU.mult))
            c = col("c_u")
            link(V.reciprocal(c, col("a_q")))
            for name in ("a_kv0", "a_kv1", "a_m"):
                link(V.reciprocal(col("inv"), col(name)))
                times(c, c, col("inv"))
            times(c, c, 1.0 / (N * DH))

            dve.wait_ge(S("b1_in"), 16)
            dve.wait_ge(S("bo_in"), 16)
            link(V.tensor_tensor(b_out, b_out, TMP[:, 1, :], ALU.add))

            def u_dve(t, j, split_too=True, first=False):
                dve.wait_ge(S("u_ps"), t + 1)
                dve.wait_ge(S(f"x_in{j}"), 80 + 8 * (t - j) + 16)
                wait(dve, "u", t)
                V.scalar_tensor_tensor(TMP[:, 0, :], banks(2 * j), c, XIN[:, j, :],
                                       ALU.mult, ALU.add).then_inc(S("u_t"), 1)
                dve.wait_ge(S("u_t"), t + 1)
                if not first:
                    dve.wait_ge(S(f"u_out{j}"), 8 * (t - j))
                V.tensor_tensor(u_out[:, j, :], TMP[:, 0, :], b_out, ALU.add).then_inc(S("u"), 1)
                if split_too:
                    split_chunk(weight(S0), t, j, 24 + t, at("s", WN0))

            u_dve(0, 0, first=True)
            u_dve(1, 1, first=True)
            steps(dve, 2, 8, u_dve)
            u_dve(8, 0, False)
            u_dve(9, 1, False)

            dve.wait_ge(S("bounds"), 2)
            dve.wait_ge(S("edges_f"), 2)
            dve.wait_ge(S("iota"), 1)
            dve.wait_ge(S("u_ps"), NT)
            made = dve.alloc_register("made")
            dve.reg_mov(made, 0)
            for b in range(NT):
                first = dve.value_load(bnd[0:1, 0, b:b + 1], min_val=0, max_val=EC - 1)
                last = dve.value_load(bnd[0:1, 1, b:b + 1], min_val=1, max_val=EC)
                with dve.Fori(first, last) as c_:
                    n = dve.snap(made)
                    slot = n % RING
                    dve.wait_ge(S("hot_free"), n + 1)
                    V.tensor_scalar(hot_src[:, slot, :], iota, srcf[:, bass.ds(c_, 1)], None,
                                    ALU.is_equal).then_inc(S("hot_src"), 1)
                    V.tensor_scalar(hot_dst[:, slot, :], iota[:, b * P:(b + 1) * P], dstf[:, bass.ds(c_, 1)], None,
                                    ALU.is_equal).then_inc(S("hot_dst"), 1)
                    dve.reg_add(made, made, 1)

            def z_dve(name, t, j, scale):
                dve.wait_ge(S(name + "_hi"), t + 1)
                V.scalar_tensor_tensor(Z[:, 1, t, :], banks(2 * j), scale, Z[:, 0, t, :],
                                       ALU.mult, ALU.subtract).then_inc(S(name + "_lo"), 1)

            def z0_dve(t, j):
                split_chunk(weight(S1), t, j, 32 + t, at("s", WS0))
                z_dve("z0", t, j, Z0_SCALE)

            steps(dve, 0, 8, z0_dve)
            for t in range(8, NT):
                z_dve("z0", t, t % 2, Z0_SCALE)
            dve.wait_ge(S("a_row"), NT)
            deg = col("deg")
            link(V.tensor_scalar(deg, deg, 1.0, None, ALU.max))
            link(V.reciprocal(deg, deg))
            dve.wait_ge(S("b0_in"), 16)
            b0s = XIN[:, 1, :]
            a = col("a_h")
            link(V.tensor_reduce(a, b0s, AXX, ALU.max, apply_absolute_value=True))
            link(V.scalar_tensor_tensor(a, at("p", WS0), 2.0 ** 6, a, ALU.mult, ALU.add))
            link(V.scalar_tensor_tensor(a, at("p", WN0), 2.0 ** 6, a, ALU.mult, ALU.add))
            range_scale(a, a)
            link(V.tensor_scalar(b0s, b0s, a, None, ALU.mult))
            times(col("c_h"), at("p", WS0), a, 1.0 / XW)
            times(col("tmp"), at("p", WN0), a, 1.0 / (XW * Z0_SCALE))
            times(col("deg_h"), deg, col("tmp"))

            def quantize(w, t, n, first=False):
                q8, above = q8_of[w]
                dve.wait_ge(S(f"stream_in{n}"), 28 * 16 + 128 * w + 16 * t + 16)
                wait(dve, "quantized", 32 * w + 4 * t + n)
                alone(dve)
                V.tensor_scalar(above, STREAM[:, n, :], col("thr")[:, w:w + 1], None,
                                ALU.is_gt, saturate=False).then_inc(S("above"), 1)
                dve.wait_ge(S("above"), 32 * w + 4 * t + n + 1)
                if not (first and n < 2):
                    dve.wait_ge(S(f"q8_out{n % 2}"), 256 * w + 32 * t + 16 * (n // 2))
                alone(dve)
                V.scalar_tensor_tensor(q8[:, n % 2, :], STREAM[:, n, :], col("nthr")[:, w:w + 1], above,
                                       ALU.is_lt, ALU.subtract, saturate=False).then_inc(S("quantized"), 1)

            def hT_dve(t):
                dve.wait_ge(S("hT_ps"), 2 * t + 2)
                V.tensor_copy(XH[:, 1, :, tile_of(t)], turned(7)).then_inc(S("hT_lo"), 1)

            def h_dve(t, j, quant=True, turn=True, first=False):
                if quant:
                    split_chunk(weight(S0), t, j, 40 + t, at("s", WN1))
                    for n in range(2):
                        quantize(0, t, n, first)
                if turn:
                    hT_dve(t - 1)
                dve.wait_ge(S("g0_ps"), t + 1)
                wait(dve, "h_lo", t)
                V.scalar_tensor_tensor(TMP[:, 0, :], banks(0), at("deg_h", t), b0s,
                                       ALU.mult, ALU.add).then_inc(S("h_t1"), 1)
                if quant:
                    for n in range(2, 4):
                        quantize(0, t, n)
                dve.wait_ge(S("s0_ps"), t + 1)
                dve.wait_ge(S("h_t1"), t + 1)
                V.scalar_tensor_tensor(TMP[:, 1, :], banks(2), col("c_h"), TMP[:, 0, :],
                                       ALU.mult, ALU.add).then_inc(S("h_t2"), 1)
                dve.wait_ge(S("h_hi"), t + 1)
                V.scalar_tensor_tensor(HL[:, j, 1, :], TMP[:, 1, :], 0.0, HL[:, j, 0, :],
                                       ALU.max, ALU.subtract).then_inc(S("h_lo"), 1)

            h_dve(0, 0, turn=False, first=True)
            h_dve(1, 1)
            steps(dve, 2, 8, h_dve)
            h_dve(8, 0, False)
            h_dve(9, 1, False)
            hT_dve(9)

            dve.wait_ge(S("h_sq"), NT)
            V.tensor_reduce(col("sq_h"), col("h_sq"), AXX, ALU.add).then_inc(S("sq"), 1)
            dve.wait_ge(S("norm"), 5)
            f = col("f_z1")
            pow2(f, col("norm_h"))
            link(V.reciprocal(f, f))
            V.tensor_scalar(f, f, 0.5, None, ALU.mult).then_inc(S("f_z1"), 1)
            dve.wait_ge(S("f_z1"), 1)
            link(V.reciprocal(col("inv"), col("a_h")))
            times(col("c_x"), at("p", WS1), col("inv"), 1.0 / W_SCALE)
            times(col("tmp"), at("p", WN1), col("inv"), 1.0 / W_SCALE)
            link(V.reciprocal(col("inv"), f))
            times(col("tmp"), col("tmp"), col("inv"))
            times(col("deg_x"), deg, col("tmp"))

            def z1_dve(t, j):
                split_chunk(weight(S1), t, j, 48 + t, at("s", WS1))
                z_dve("z1", t, j, f)

            steps(dve, 0, 8, z1_dve)
            for t in range(8, NT):
                z_dve("z1", t, t % 2, f)

            def x2T_dve(t):
                dve.wait_ge(S("x2T_ps"), t + 1)
                V.tensor_copy(x2T[:, :, tile_of(t)], turned(6)).then_inc(S("x2T"), 1)

            def x1_dve(t, j, quant=True, turn=True, first=False):
                if turn:
                    x2T_dve(t - 1)
                dve.wait_ge(S("g1_ps"), t + 1)
                dve.wait_ge(S(f"x_in{j}"), 160 + 8 * (t - j) + 16)
                wait(dve, "r", t)
                V.scalar_tensor_tensor(TMP[:, 0, :], banks(0), at("deg_x", t), XIN[:, j, :],
                                       ALU.mult, ALU.add).then_inc(S("x1_t1"), 1)
                if quant:
                    for n in range(4):
                        quantize(1, t, n)
                dve.wait_ge(S("s1_ps"), t + 1)
                dve.wait_ge(S("x1_t1"), t + 1)
                if not first:
                    dve.wait_ge(S("x1_out"), 16 * t)
                V.scalar_tensor_tensor(TMP[:, 1, :], banks(2), col("c_x"), TMP[:, 0, :],
                                       ALU.mult, ALU.add).then_inc(S("x1"), 1)
                dve.wait_ge(S("x1"), t + 1)
                for n in range(2):
                    V.bn_stats(st[:, 6 * n:6 * n + 6], TMP[:, 1, n * 512:(n + 1) * 512]).then_inc(S("y_stats"), 1)
                dve.wait_ge(S("y_stats"), 2 * t + 2)
                alone(dve)
                V.bn_aggr(mv[:, :], st[:, :]).then_inc(S("y_mv"), 1)
                dve.wait_ge(S("y_std"), t + 1)
                V.reciprocal(col("y_rstd"), col("y_std")).then_inc(S("y_rstd"), 1)
                dve.wait_ge(S("y_rstd"), t + 1)
                V.tensor_scalar(x2n, TMP[:, 1, :], mv[:, 0:1], col("y_rstd"),
                                ALU.subtract, ALU.mult).then_inc(S("x2n"), 1)
                dve.wait_ge(S("x2n"), t + 1)
                V.tensor_reduce(col("y_max"), x2n, AXX, ALU.max, apply_absolute_value=True).then_inc(S("y_max"), 1)
                dve.wait_ge(S("y_max"), t + 1)
                V.tensor_scalar(col("y_clip"), col("y_max"), EPS_Q, None, ALU.max).then_inc(S("y_clip"), 1)
                dve.wait_ge(S("y_clip"), t + 1)
                V.tensor_scalar(at("dq1", t), col("y_clip"), col("nsw")[:, 0:1], None,
                                ALU.mult).then_inc(S("dq1"), 1)
                V.reciprocal(col("y_inv"), col("y_clip")).then_inc(S("y_inv"), 1)
                dve.wait_ge(S("y_inv"), t + 1)
                V.tensor_scalar(col("y_sc"), col("y_inv"), 127.0, None, ALU.mult).then_inc(S("y_sc"), 1)
                dve.wait_ge(S("r_magic"), t + 1)
                V.tensor_scalar(r_rows[:, j, :], x2n, -MAGIC, None, ALU.add).then_inc(S("r"), 1)

            x1_dve(0, 0, turn=False, first=True)
            x1_dve(1, 1)
            steps(dve, 2, 8, x1_dve)
            x1_dve(8, 0, False)
            x1_dve(9, 1, False)
            x2T_dve(9)

            def hid_max(t, slot):
                wait(dve, "g_sc", t)
                wait(dve, "y", t - 1)
                for n in range(4):
                    dve.wait_ge(S("gelu"), 8 * t + 2 * n + 2)
                    V.tensor_reduce(AM[:, n:n + 1], hid[:, slot, n * D:(n + 1) * D], AXX, ALU.max,
                                    apply_absolute_value=True).then_inc(S("g_part"), 1)
                dve.wait_ge(S("g_part"), 4 * t + 4)
                V.tensor_reduce(col("g_max"), AM[:, :], AXX, ALU.max).then_inc(S("g_max"), 1)
                dve.wait_ge(S("g_max"), t + 1)
                V.tensor_scalar(col("g_clip"), col("g_max"), EPS_Q, None, ALU.max).then_inc(S("g_clip"), 1)
                dve.wait_ge(S("g_clip"), t + 1)
                V.tensor_scalar(at("dq2", slot), col("g_clip"), col("nsw")[:, 1:2], None,
                                ALU.mult).then_inc(S("dq2"), 1)
                V.reciprocal(col("g_inv"), col("g_clip")).then_inc(S("g_inv"), 1)
                dve.wait_ge(S("g_inv"), t + 1)
                V.tensor_scalar(col("g_sc"), col("g_inv"), 127.0, None, ALU.mult).then_inc(S("g_sc"), 1)

            def ffn_dve(t, j, more=True, first=False):
                if not first:
                    dve.wait_ge(S("gT_ps"), 4 * t)
                for n in range(4):
                    dve.wait_ge(S("g_magic"), 4 * t + n + 1)
                    V.tensor_scalar(hid_q[:, n * D:(n + 1) * D], hid[:, j, n * D:(n + 1) * D], -MAGIC, None,
                                    ALU.add).then_inc(S("g_q"), 1)
                if more:
                    hid_max(t + 1, 1 - j)
                for n in (1, 3):
                    dve.wait_ge(S("gT_ps"), 4 * t + n + 1)
                    V.tensor_copy(hid_T[:, j, 8 * n:8 * n + 8, :], turned(7)).then_inc(S("gT_lo"), 1)
                dve.wait_ge(S("f2_ps"), t + 1)
                dve.wait_ge(S(f"x1_in{j}"), 8 * (t - j) + 16)
                dve.wait_ge(S("dq2"), t + 1)
                if not first:
                    dve.wait_ge(S(f"y_out{j}"), 8 * (t - j))
                V.scalar_tensor_tensor(y_out[:, j, :], banks(4), at("dq2", j), x1_in[:, j, :],
                                       ALU.mult, ALU.add).then_inc(S("y"), 1)

            hid_max(0, 0)
            ffn_dve(0, 0, first=True)
            ffn_dve(1, 1)
            steps(dve, 2, 8, ffn_dve)
            ffn_dve(8, 0)
            ffn_dve(9, 1, False)

        @block.tensor
        def _(pe):
            mm = nc.tensor.matmul

            def product(acc, left, right, ready=None):
                for kc in range(KC):
                    if ready is not None:
                        pe.wait_ge(S("split_lo"), ready + kc + 1)
                    for l, rs in ((0, (0, 1)), (1, (0,))):
                        for r in rs:
                            for n in range(2):
                                last = mm(acc[:, n * BANK:(n + 1) * BANK], left(l, kc),
                                          right(kc, r)[:, n * BANK:(n + 1) * BANK],
                                          start=(kc == 0 and l == 0 and r == 0), stop=(kc == KC - 1 and l == 1))
                return last

            def turn(bank, pieces, n=8):
                for k in range(n):
                    last = nc.tensor.transpose(turned(bank)[:, k, :], pieces(k), ident[:, :])
                return last

            def total(count, src, n):
                mm(ps[:, NORM_AT[count]:NORM_AT[count] + n], ones[:, :], src, start=True, stop=True).then_inc(S("norm_ps"), 1)

            def xT_pe(t, j):
                wait(pe, "xT_hi", t)
                wait(pe, "xT_lo", t)
                pe.wait_ge(S("ln_hi"), t + 1)
                turn(2, lambda k: HL[:, j, 0, k * P:(k + 1) * P]).then_inc(S("xT_ps"), 1)
                pe.wait_ge(S("ln_lo"), t + 1)
                turn(3, lambda k: HL[:, j, 1, k * P:(k + 1) * P]).then_inc(S("xT_ps"), 1)

            def of_x(t):
                return lambda l, kc: XH[:, l, kc, tile_of(t)]

            def of(w):
                return lambda kc, r: w[:, kc, r, :]

            def kv_sum(t, j, first=False, last_rows=P):
                pe.wait_ge(S("k_lo"), t + 1)
                pe.wait_ge(S("v_lo"), t + 1)
                for p in range(KC):
                    c = slice(P * p, P * p + P)
                    for n, (a, b) in enumerate(((2, 0), (2, 1), (3, 0))):
                        last = mm(ps[:, 6 * BANK + P * p:6 * BANK + P * p + P], kv[0:last_rows, j, a, c],
                                  kv[0:last_rows, j, b, c], start=(first and n == 0 and p % 4 == 0),
                                  stop=(last_rows != P and n == 2), skip_group_check=True)
                last.then_inc(S("kv_ps"), 1)

            def k_pe(t, ready=None):
                wait(pe, "k_t", t)
                pe.wait_ge(S("xT_hi"), t + 1)
                pe.wait_ge(S("xT_lo"), t + 1)
                product(banks(0), of_x(t), of(Wk_s), ready).then_inc(S("k_ps"), 1)

            def v_pe(t, ready=None):
                wait(pe, "v_t", t)
                product(banks(4), of_x(t), of(Wv_s), ready).then_inc(S("v_ps"), 1)

            def kv_pe(t, j):
                k_pe(t)
                kv_sum(t - 1, 1 - j)
                xT_pe(t + 1, 1 - j)
                v_pe(t)

            pe.wait_ge(S("ident"), 1)
            xT_pe(0, 0)
            pe.wait_ge(S("ones"), 1)
            pe.wait_ge(S("sq"), 1)
            total(1, col("sq0"), 1)
            k_pe(0, ready=0)
            xT_pe(1, 1)
            pe.wait_ge(S("sq"), 2)
            total(2, col("sq1"), 1)
            v_pe(0, ready=8)
            k_pe(1)
            kv_sum(0, 0, first=True)
            xT_pe(2, 0)
            v_pe(1)
            steps(pe, 2, 8, lambda t, j: kv_pe(t, j))
            kv_pe(8, 0)
            k_pe(9)
            kv_sum(8, 0)
            pe.wait_ge(S("sq"), 4)
            pe.wait_ge(S("xT_hi"), NT)
            total(3, col("sq6"), 7)
            v_pe(9)

            def q_pe(m, j):
                wait(pe, "q_t", m - 1)
                mc = bass.ds(m * P, P)
                for kc in range(KC):
                    for l, rs in ((0, (0, 1)), (1, (0,))):
                        for r in rs:
                            for a in range(0, NP_, BANK):
                                b = min(a + BANK, NP_)
                                last = mm(ps[:, 3 * j * BANK + a:3 * j * BANK + b], Wq_s[:, kc, l, mc],
                                          XH[:, r, kc, a:b], start=(kc == 0 and l == 0 and r == 0),
                                          stop=(kc == KC - 1 and l == 1))
                last.then_inc(S("q_ps"), 1)

            pe.wait_ge(S("split_lo"), 24)
            pe.wait_ge(S("k_t"), NT)
            q_pe(0, 0)
            pe.wait_ge(S("v_t"), NT)
            kv_sum(9, 1, last_rows=N - (NT - 1) * P)
            q_pe(1, 1)
            steps(pe, 2, 8, q_pe)

            pe.wait_ge(S("kv_sq"), 1)
            pe.wait_ge(S("q_lo"), 8)
            total(4, col("kv_sq"), 1)
            pe.wait_ge(S("wo_in"), 16)
            for p in range(KC):
                if p >= 3:
                    pe.wait_ge(S("m_lo"), p - 2)
                for n in range(2):
                    last = mm(ps[:, (2 * (p % 3) + n) * BANK:(2 * (p % 3) + n + 1) * BANK], kvT[:, P * p:P * p + P],
                              Wo_raw[:, p, n * BANK:(n + 1) * BANK], start=True, stop=True)
                last.then_inc(S("m_ps"), 1)
            pe.wait_ge(S("sq"), 5)
            mm(ps[:, MEAN_AT:MEAN_AT + 2], ones[:, :], col("w_sum"), start=True, stop=True).then_inc(S("mean_ps"), 1)

            pe.wait_ge(S("m_lo"), KC)

            def u_pe(t, j):
                wait(pe, "u_t", t - 1)
                product(banks(2 * j), lambda l, p: qT[:, l, p, tile_of(t)], of(M_s)).then_inc(S("u_ps"), 1)

            u_pe(0, 0)
            u_pe(1, 1)
            steps(pe, 2, NT, u_pe)

            pe.wait_ge(S("u_t"), NT)
            pe.sem_inc(S("hot_free"), RING)
            done = pe.alloc_register("done")
            pe.reg_mov(done, 0)

            def aT_pe(b):
                pe.wait_ge(S("a_row"), b + 1)
                if b >= 1:
                    pe.wait_ge(S("aT_hi"), b)
                    pe.wait_ge(S("aT_lo"), b)
                turn(6, lambda k: a_row[:, b % 2, k * P:(k + 1) * P]).then_inc(S("aT_ps"), 1)
                turn(7, lambda k: a_row[:, b % 2, (8 + k) * P:(9 + k) * P], NT - 8).then_inc(S("aT_ps"), 1)

            pe.wait_ge(S("zero"), 1)
            pe.wait_ge(S("iota"), 1)
            pe.wait_ge(S("bounds"), 2)
            for b in range(NT):
                first = pe.value_load(bnd[0:1, 0, b:b + 1], min_val=0, max_val=EC - 1)
                last = pe.value_load(bnd[0:1, 1, b:b + 1], min_val=1, max_val=EC)
                parts = [(a, min(a + BANK, NP_)) for a in range(0, NP_, BANK)]
                acc = banks(3 * (b % 2), cut=NP_)
                wait(pe, "a_row", b - 1)
                for a, z in parts:
                    mm(acc[:, a:z], zero[:, :], iota[:, a:z], start=True, stop=False, skip_group_check=True)
                with pe.Fori(first, last):
                    n = pe.snap(done)
                    slot = n % RING
                    pe.wait_ge(S("hot_src"), n + 1)
                    pe.wait_ge(S("hot_dst"), n + 1)
                    for a, z in parts:
                        one = mm(acc[:, a:z], hot_dst[:, slot, :], hot_src[:, slot, a:z], start=False, stop=False,
                                 skip_group_check=True)
                    one.then_inc(S("hot_free"), 1)
                    pe.reg_add(done, done, 1)
                for a, z in parts:
                    one = mm(acc[:, a:z], zero[:, :], iota[:, a:z], start=False, stop=True, skip_group_check=True)
                one.then_inc(S("a_ps"), 1)
                if b >= 1:
                    aT_pe(b - 1)
            aT_pe(NT - 1)

            pe.wait_ge(S("split_lo"), 32)

            def z0_pe(t, j):
                wait(pe, "z0_lo", t - 1)
                product(banks(2 * j), of_x(t), of(weight(S0))).then_inc(S("z0_ps"), 1)

            z0_pe(0, 0)
            z0_pe(1, 1)
            steps(pe, 2, NT, z0_pe)

            def edge_sum(t, name):
                for s in range(NT):
                    for r in range(2):
                        for n in range(2):
                            last = mm(ps[:, n * BANK:(n + 1) * BANK], ATv[:, s, tile_of(t)],
                                      Z[:, r, s, n * BANK:(n + 1) * BANK], start=(s == 0 and r == 0),
                                      stop=(s == NT - 1 and r == 1))
                last.then_inc(S(name), 1)

            def hT_pe(t, j):
                wait(pe, "hT_hi", t)
                wait(pe, "hT_lo", t)
                pe.wait_ge(S("h_hi"), t + 1)
                turn(6, lambda k: HL[:, j, 0, k * P:(k + 1) * P]).then_inc(S("hT_ps"), 1)
                pe.wait_ge(S("h_lo"), t + 1)
                turn(7, lambda k: HL[:, j, 1, k * P:(k + 1) * P]).then_inc(S("hT_ps"), 1)

            def h_pe(t, j, turn_too=True):
                wait(pe, "h_t1", t)
                edge_sum(t, "g0_ps")
                if turn_too:
                    hT_pe(t - 1, 1 - j)
                wait(pe, "h_t2", t)
                product(banks(2), of_x(t), of(weight(S1))).then_inc(S("s0_ps"), 1)

            pe.wait_ge(S("aT_hi"), NT)
            pe.wait_ge(S("aT_lo"), NT)
            pe.wait_ge(S("z0_hi"), NT)
            pe.wait_ge(S("z0_lo"), NT)
            pe.wait_ge(S("split_lo"), 40)
            h_pe(0, 0, False)
            h_pe(1, 1)
            steps(pe, 2, NT, h_pe)

            def z1_pe(t, j):
                wait(pe, "z1_lo", t - 1)
                product(banks(2 * j), of_x(t), of(weight(S0))).then_inc(S("z1_ps"), 1)

            pe.wait_ge(S("split_lo"), 48)
            pe.wait_ge(S("hT_hi"), NT - 1)
            pe.wait_ge(S("hT_lo"), NT - 1)
            pe.wait_ge(S("h_t1"), NT)
            z1_pe(0, 0)
            hT_pe(NT - 1, 1)
            pe.wait_ge(S("hT_hi"), NT)
            pe.wait_ge(S("hT_lo"), NT)
            pe.wait_ge(S("sq"), 6)
            total(5, col("sq_h"), 1)
            pe.wait_ge(S("h_t2"), NT)
            z1_pe(1, 1)
            steps(pe, 2, NT, z1_pe)

            def x2T_pe(t, j):
                wait(pe, "x2T", t)
                pe.wait_ge(S("r"), t + 1)
                turn(6, lambda k: r_rows[:, j, k * P:(k + 1) * P]).then_inc(S("x2T_ps"), 1)

            def x1_pe(t, j, turn_too=True):
                wait(pe, "x1_t1", t)
                edge_sum(t, "g1_ps")
                if turn_too:
                    x2T_pe(t - 1, 1 - j)
                wait(pe, "x1", t)
                product(banks(2), of_x(t), of(weight(S1))).then_inc(S("s1_ps"), 1)

            pe.wait_ge(S("z1_hi"), NT)
            pe.wait_ge(S("z1_lo"), NT)
            pe.wait_ge(S("split_lo"), 56)
            x1_pe(0, 0, False)
            x1_pe(1, 1)
            steps(pe, 2, NT, x1_pe)

            def f1_pe(t, j):
                pe.wait_ge(S("x2_tile"), t + 1)
                for n in range(8):
                    wait(pe, "gelu", 8 * t + n - 3)
                    alone(pe)
                    for kc in range(KC):
                        last = mm(banks(n % 4, 1), x2_tile[:, j, kc, :], w1q[:, kc, n * BANK:(n + 1) * BANK],
                                  start=(kc == 0), stop=(kc == KC - 1))
                    last.then_inc(S("f1_ps"), 1)

            def gT_pe(t, j, n):
                wait(pe, "gT_lo" if n % 2 else "gT_hi", 2 * t + n // 2)
                pe.wait_ge(S("g_q"), 4 * t + n + 1)
                turn(6 + n % 2, lambda k: hid_q[:, (8 * n + k) * P:(8 * n + k + 1) * P]).then_inc(S("gT_ps"), 1)

            def f2_pe(t, j, n):
                pe.wait_ge(S("gT_lo" if n % 2 else "gT_hi"), 2 * t + n // 2 + 1)
                alone(pe)
                for kc in range(8 * n, 8 * n + 8):
                    for h in range(2):
                        last = mm(banks(4 + h, 1), hid_T[:, j, kc, :], w2q[:, kc, h * BANK:(h + 1) * BANK],
                                  start=(kc == 0), stop=(kc == HC - 1))
                return last

            def out_pe(t, j):
                gT_pe(t, j, 0)
                gT_pe(t, j, 1)
                wait(pe, "y", t)
                f2_pe(t, j, 0)
                gT_pe(t, j, 2)
                f2_pe(t, j, 1)
                gT_pe(t, j, 3)
                f2_pe(t, j, 2)
                f2_pe(t, j, 3).then_inc(S("f2_ps"), 1)

            def ffn_pe(t, j):
                f1_pe(t + 1, 1 - j)
                out_pe(t, j)

            pe.wait_ge(S("w1q_in"), 16)
            pe.wait_ge(S("x1_t1"), NT)
            pe.wait_ge(S("x1"), NT)
            f1_pe(0, 0)
            x2T_pe(NT - 1, 1)
            pe.wait_ge(S("x2T"), NT)
            pe.wait_ge(S("w2q_in"), 16)
            ffn_pe(0, 0)
            ffn_pe(1, 1)
            steps(pe, 2, 8, ffn_pe)
            ffn_pe(8, 0)
            out_pe(9, 1)


def kernel(**inputs):
    import numpy as np
    import concourse.bacc as bacc
    from concourse.bass_utils import run_bass_kernel_spmd

    a = {k: np.asarray(v) for k, v in inputs.items()}
    x = np.zeros((NP_, D), np.float32)
    x[:N] = a["x"]
    src = np.full(EC * P, 2 * NP_, np.int32)
    src[:NE] = a["src"]
    dst = np.full(EC * P, NP_ - 1, np.int32)
    dst[:NE] = a["dst"]
    dst_rows = np.full((2 * P, P), 4 * NP_, np.int32)
    dst_rows[:EC] = dst.reshape(EC, P)
    arrays = dict(
        x=x, src_cols=src.reshape(EC, P).T, dst_cols=dst.reshape(EC, P).T, dst_rows=dst_rows,
        Wself0=a["L0_gnn_W_self0"], Wneigh0=a["L0_gnn_W_neigh0"], b0=a["L0_gnn_b0"],
        Wself1=a["L0_gnn_W_self1"], Wneigh1=a["L0_gnn_W_neigh1"], b1=a["L0_gnn_b1"],
        Wq=a["L0_mix_Wq"], bq_cols=a["L0_mix_bq"].reshape(KC, P).T, Wk=a["L0_mix_Wk"], bk=a["L0_mix_bk"],
        Wv=a["L0_mix_Wv"], bv=a["L0_mix_bv"], Wo=a["L0_mix_Wo"], bo=a["L0_mix_bo"],
        w1t=a["L0_ffn_w1"].T, w2t=a["L0_ffn_w2"].T)
    arrays = {k: np.ascontiguousarray(v) for k, v in arrays.items()}
    nc = bacc.Bacc("TRN2", target_bir_lowering=False, num_devices=1, dynamic_dma_scratch_size=1024)
    args = {k: nc.dram_tensor(f"in_{k}", v.shape, mybir.dt.from_np(v.dtype), kind="ExternalInput").ap()
            for k, v in arrays.items()}
    out = nc.dram_tensor("out", (NP_, D), F32, kind="ExternalOutput").ap()
    gps_kernel(nc, **args, out=out)
    r = run_bass_kernel_spmd(nc, [{f"in_{k}": v for k, v in arrays.items()}], core_ids=[0])
    return r.results[0]["out"][:N]
```

```python
from contextlib import ExitStack

import concourse.bass as bass
from concourse import mybir

F32, F16, F8, I32 = mybir.dt.float32, mybir.dt.float16, mybir.dt.float8e4, mybir.dt.int32
ACT = mybir.ActivationFunctionType
ALU = mybir.AluOpType
AXX = mybir.AxisListType.X
RMAX = bass.bass_isa.ReduceOp.max

P = 128
N = 1250
NT = -(-N // P)
NP_ = NT * P
D = 1024
KC = D // P
HID = 4 * D
HC = HID // P
DH = 64
NE = 20000
EC = -(-NE // P)
BANK = 512
QUAD = 4
ECP = EC + 2 * QUAD
EPS_LN, EPS_Q = 1e-5, 1e-5
MAGIC = 1.5 * 2.0 ** 23
TINY = 2.0 ** -60
POW2_MASK = 0x7F800000
X_SCALE = 2.0 ** 10
W_SCALE = 2.0 ** 14
XW = X_SCALE * W_SCALE
Z0_SCALE = 2.0 ** -15
NORMS, KV_MEANS = 6, 2
Q_MEANS, U_MEANS = 4, 2
Q_FIRST = 8 * KV_MEANS
U_FIRST = Q_FIRST + KC * Q_MEANS
WK, WV, WQ, WO, WN0, WS0, WN1, WS1 = range(8)
NORM_AT = {1: 6 * BANK, 2: 7 * BANK, 3: 2 * BANK, 4: 2 * BANK, 5: 6 * BANK, 6: 6 * BANK}
MEAN_AT = 4 * BANK
M_BANK = {5: 4, 6: 2, 7: 6}


def gps_kernel(nc, x, src_cols, dst_cols, dst_rows, Wself0, Wneigh0, b0, Wself1, Wneigh1, b1,
               Wq, bq_cols, Wk, bk, Wv, bv, Wo, bo, w_all, w1t, w2t, out):
    ctx = ExitStack()
    with ctx:
        def sb(name, shape, dt):
            return ctx.enter_context(nc.sbuf_tensor(name, shape, dt))

        named = {}

        def S(name):
            if name not in named:
                named[name] = ctx.enter_context(nc.semaphore(name))
            return named[name]

        XH = sb("XH", [P, 2, KC, NP_], F16)
        Zb = sb("Zb", [P, 2 * NT * D], F16)
        S0 = sb("S0", [P, 2 * KC * D], F16)
        S1 = sb("S1", [P, 2 * KC * D], F16)
        AT = sb("AT", [P, NT * NP_], F16)
        STREAM = sb("STREAM", [P, 4, D], F32)
        SPLIT = sb("SPLIT", [P, 2, D], F32)
        XIN = sb("XIN", [P, 2, D], F32)
        TMP = sb("TMP", [P, 2, D], F32)
        HL = sb("HL", [P, 2, 2, D], F16)
        ident = sb("ident", [P, P], F16)
        zero = sb("zero", [P, P], F16)
        ones = sb("ones", [P, P], F32)
        srcf = sb("srcf", [P, ECP], F32)
        dstf = sb("dstf", [P, ECP], F32)
        bnd = sb("bnd", [P, 2, NT], I32)
        NPW = sb("NPW", [P, 8, KC], F32)
        MW = sb("MW", [P, 2, HC], F32)
        st = sb("st", [P, 12], F32)
        mv = sb("mv", [P, 2], F32)
        AM = sb("AM", [P, 4], F32)
        widths = dict(
            magic=1, eps=1, first=NT, chunk1=2, chunk_left=2,
            ln_std=1, ln_rstd=1, p=8, s=8, sq0=1, sq1=1, norm_kv0=1, norm_kv1=1, a_kv0=1, a_kv1=1, c_kv0=1, c_kv1=1,
            sq_q=2, norm_q=2, sq5=5, norm5=5, bq=KC, bq2=KC, bqs=KC, a_q=1, c_q=1, kv_sq=1, norm_m=1, a_m=1,
            c_u=1, inv=1, tmp=1,
            w_sum=2, w_mean=2, thr=2, nthr=2, nsw=2, deg=NT, deg_h=NT, deg_x=NT, a_h=1, c_h=1, c_x=1,
            h_sq=NT, sq_h=1, norm_h=1, f_z1=1, y_std=1, y_rstd=1, y_max=1, y_clip=1, y_inv=1, y_sc=1, dq1=NT,
            g_max=1, g_clip=1, g_inv=1, g_sc=1, dq2=2)
        first_col, n_cols = {}, 0
        for name, n in widths.items():
            first_col[name] = n_cols
            n_cols += n
        cols = sb("cols", [P, n_cols], F32)

        def col(name):
            return cols[:, first_col[name]:first_col[name] + widths[name]]

        def at(name, i):
            return cols[:, bass.ds(i + first_col[name], 1)]

        ps = ctx.enter_context(nc.psum_tensor("ps", [P, 8 * BANK], F32))

        def banks(a, n=2, cut=None):
            return ps[:, a * BANK:a * BANK + (cut or n * BANK)]

        def turned(bank):
            return ps[:, bank * BANK:(bank + 1) * BANK].bitcast(F16).rearrange("p (k n) -> p k n", n=P)

        def weight(region):
            return region[:, 0:2 * KC * D].rearrange("p (k h n) -> p k h n", k=KC, h=2)

        Wk_s, Wv_s, Wq_s, M_s = weight(Zb), weight(S1), weight(S0), weight(S1)
        raw = S0[:, :].bitcast(F32).rearrange("p (k n) -> p k n", k=KC)
        Wv_tail = Zb[:, 2 * KC * D:2 * KC * D + 4 * D].bitcast(F32).rearrange("p (k n) -> p k n", k=2)
        Wo_raw = S1[:, :].bitcast(F32).rearrange("p (k n) -> p k n", k=KC)
        qT = Zb[:, :].rearrange("p (h k n) -> p h k n", h=2, k=KC)
        Z = Zb[:, :].rearrange("p (h t n) -> p h t n", h=2, t=NT)
        stream16 = STREAM[:, :, :].rearrange("p a n -> p (a n)").bitcast(F16)
        hot_src = stream16[:, 0:QUAD * NP_].rearrange("p (r n) -> p r n", r=QUAD)
        hot_dst = stream16[:, QUAD * NP_:QUAD * (NP_ + P)].rearrange("p (r n) -> p r n", r=QUAD)
        a_row = stream16[:, QUAD * (NP_ + P):QUAD * (NP_ + P) + NP_]
        iota = HL[:, :, :, :].rearrange("p a b n -> p (a b n)")[:, 0:NP_]
        kv = AT[:, 0:8 * D].rearrange("p (r q n) -> p r q n", r=2, q=4)
        b_kv = AT[:, 8 * D:12 * D].bitcast(F32).rearrange("p (a n) -> p a n", a=2)
        q_t = AT[:, 0:4 * NP_].bitcast(F32).rearrange("p (r n) -> p r n", r=2)
        edges = AT[:, 5 * D:5 * D + 4 * ECP].bitcast(I32).rearrange("p (a c) -> p a c", a=2)
        d_int = AT[:, 6 * D:6 * D + 512].bitcast(I32).rearrange("p (g e) -> p g e", g=2)
        d_flt = AT[:, 6 * D + 512:7 * D].bitcast(F32).rearrange("p (g e) -> p g e", g=2)
        blk = AT[:, 7 * D:7 * D + 512].bitcast(F32)
        kvT = AT[:, 8 * D:10 * D].bitcast(F32)
        b_out = AT[:, 10 * D:12 * D].bitcast(F32)
        u_out = AT[:, 0:4 * D].bitcast(F32).rearrange("p (r n) -> p r n", r=2)
        ATv = AT[:, :].rearrange("p (s n) -> p s n", s=NT)
        x1_in = AT[:, 0:4 * D].bitcast(F32).rearrange("p (r n) -> p r n", r=2)
        y_out = AT[:, 4 * D:8 * D].bitcast(F32).rearrange("p (r n) -> p r n", r=2)
        w1q = S0[:, :].bitcast(F8)[:, 0:KC * HID].rearrange("p (k n) -> p k n", k=KC)
        w2q = S1[:, :].bitcast(F8)[:, 0:HC * D].rearrange("p (k n) -> p k n", k=HC)
        r_rows = HL[:, 0, :, :]
        x2n = HL[:, 1, :, :].rearrange("p a n -> p (a n)").bitcast(F32)
        hid = Zb[:, 0:4 * HID].bitcast(F32).rearrange("p (r n) -> p r n", r=2)
        hid_q = Zb[:, 4 * HID:5 * HID]
        hid_T = XH[:, 1, :, :].rearrange("p k n -> p (k n)")[:, 0:2 * HID].rearrange(
            "p (r k n) -> p r k n", r=2, k=HC)
        x2T = XH[:, 0, :, :]
        x2_tile = SPLIT[:, 1, :].bitcast(F16).rearrange("p (r k n) -> p r k n", r=2, k=KC)

        def ternary(region):
            v = region.bitcast(F8)
            return v[:, 0:2 * D].rearrange("p (r n) -> p r n", r=2), v[:, 2 * D:3 * D]

        q8_of = {0: ternary(XIN[:, 0, :]), 1: ternary(SPLIT[:, 0, :])}

        u_d = nc.dram_tensor("u_scratch", (NP_, D), F32, kind="Internal").ap()
        x1_d = nc.dram_tensor("x1_scratch", (NP_, D), F32, kind="Internal").ap()
        wq_d = [nc.dram_tensor(f"w{w + 1}q_scratch", (P, HC * D // 2), F16, kind="Internal").ap() for w in range(2)]

        def Wv_raw(kc):
            return STREAM[:, kc, :] if kc < 4 else SPLIT[:, kc - 4, :] if kc < 6 else Wv_tail[:, kc - 6, :]

        def wait(eng, name, count):
            if not isinstance(count, int) or count > 0:
                eng.wait_ge(S(name), count)

        def alone(eng):
            eng.sem_inc(S("alone_" + eng.engine.name), 1)

        def rows(dram, t):
            return dram[bass.ds(t * P, P), :]

        def tile_of(t):
            return bass.ds(t * P, P)

        MW_all = MW[:, :, :].rearrange("p w k -> p (w k)")
        w_flat = [w1t.rearrange("r (q n) -> (r q) n", n=D), w2t]
        NPW_all = NPW[:, :, :].rearrange("p w k -> p (w k)")

        def quant_src(w, i, j):
            if w == 0:
                return w1t[bass.ds(i * P, P), j * D:(j + 1) * D]
            return w2t[bass.ds(i * 4 * P + j * P, P), :]

        def steps(eng, a, b, body):
            assert (b - a) % 2 == 0
            with eng.Fori(0, (b - a) // 2) as pair:
                for j in range(2):
                    body(pair * 2 + (a + j), j)

        block = ctx.enter_context(nc.Block())

        @block.sync
        def _(sp):
            def load_x(t, slot):
                sp.dma_start(XIN[:, slot, :], rows(x, t)).then_inc(S(f"x_in{slot}"), 16)

            def load_split(dram, kc, slot, idx):
                sp.wait_ge(S("split_lo"), idx - 1)
                sp.dma_start(SPLIT[:, slot, :], rows(dram, kc)).then_inc(S(f"split_in{slot}"), 16)

            load_x(0, 0)
            for kc in range(KC):
                sp.dma_start(raw[:, kc, :], Wk[kc * P:(kc + 1) * P, :]).then_inc(S(f"wk_in{kc}"), 16)
                if kc == 5:
                    load_x(1, 1)
            sp.dma_start(b_kv[:, 0, :], bk.partition_broadcast(P)).then_inc(S("bk_in"), 16)
            for kc in range(KC):
                sp.dma_start(Wv_raw(kc), Wv[kc * P:(kc + 1) * P, :]).then_inc(S(f"wv_in{kc // 2}"), 16)
            sp.wait_ge(S("ln_xn"), 1)
            load_x(2, 0)
            sp.dma_start(b_kv[:, 1, :], bv.partition_broadcast(P)).then_inc(S("bv_in"), 16)
            sp.dma_start(col("bq"), bq_cols).then_inc(S("bq_in"), 16)

            def kv_loads(t, j, first=False, split=False, more=True):
                if more:
                    sp.wait_ge(S("ln_xn"), t + 1)
                    load_x(t + 2, 1 - j)
                if split:
                    for n in range(2):
                        kc = 2 * (t - 4) + n
                        load_split(Wq, kc, n, KC * WQ + kc)
                for n in range(NORMS + KV_MEANS):
                    slot = n % 4
                    if first and n < 4:
                        sp.wait_ge(S("split_lo"), KC + n + 1)
                    wait(sp, "stream_used", (NORMS + KV_MEANS) * (t - 1) + n - 3)
                    chunk = rows(w_all, NORMS * (t - 1) + n) if n < NORMS else \
                        rows(w_flat[0], KV_MEANS * (t - 1) + n - NORMS)
                    sp.dma_start(STREAM[:, slot, :], chunk).then_inc(S(f"stream_in{slot}"), 16)

            kv_loads(1, 0, first=True)
            kv_loads(2, 1)
            kv_loads(3, 0)
            steps(sp, 4, 8, lambda t, j: kv_loads(t, 1 - j, split=True))
            kv_loads(8, 1, more=False)

            sp.wait_ge(S("v_ps"), NT)
            sp.dma_start(Wo_raw, Wo.rearrange("(k p) n -> p k n", p=P)).then_inc(S("wo_in"), 16)
            sp.wait_ge(S("v_t"), NT)
            sp.wait_ge(S("kv_ps"), NT)
            sp.dma_start(edges[:, 0, :], src_cols).then_inc(S("edges_in"), 16)
            sp.dma_start(edges[:, 1, :], dst_cols).then_inc(S("edges_in"), 16)
            sp.dma_start(d_int, dst_rows.rearrange("(g p) e -> p g e", p=P)).then_inc(S("edges_in"), 16)
            sp.dma_start(b_out, b1.partition_broadcast(P)).then_inc(S("b_out_in"), 16)
            sp.dma_start(TMP[:, 1, :], bo.partition_broadcast(P)).then_inc(S("b_out_in"), 16)

            def mean_load(w, c, slot):
                sp.wait_ge(S("stream_used"), c + (8 * NORMS - 3))
                sp.dma_start(STREAM[:, slot, :], rows(w_flat[w], c - HC * w)).then_inc(S(f"stream_in{slot}"), 16)

            def mean_loads(w, first, last):
                with sp.Fori(first // 4, last // 4) as i:
                    for j in range(4):
                        mean_load(w, 4 * i + j, j)

            mean_loads(0, Q_FIRST, HC)
            mean_loads(1, HC, U_FIRST)

            sp.wait_ge(S("ln_xn"), NT)
            load_x(0, 0)
            load_x(1, 1)

            def u_moves(t, j, split=True):
                if split:
                    load_split(Wneigh0, t, j, 24 + t)
                    for n in range(U_MEANS):
                        mean_load(1, U_FIRST + U_MEANS * t + n, U_MEANS * j + n)
                sp.wait_ge(S("u"), t + 1)
                sp.dma_start(rows(u_d, t), u_out[:, j, :]).then_inc(S(f"u_out{j}"), 16)
                if split:
                    load_x(t + 2, j)

            steps(sp, 0, 8, u_moves)
            for t in range(8, NT):
                u_moves(t, t % 2, False)
            sp.dma_start(XIN[:, 1, :], b0.partition_broadcast(P)).then_inc(S("b0_in"), 16)

            sp.wait_ge(S("u_ps"), NT)
            steps(sp, 0, 8, lambda t, j: load_split(Wself0, t, j, 32 + t))

            def quant_moves(w, t, j, more=True):
                for n in range(4):
                    c = 32 * w + 4 * t + n
                    sp.wait_ge(S("quantized"), c + 1)
                    sp.dma_start(wq_d[w][:, bass.ds((4 * t + n) * (D // 2), D // 2)],
                                 q8_of[w][0][:, n % 2, :].bitcast(F16))\
                        .then_inc(S(f"q8_out{n % 2}"), 16)
                    if more:
                        sp.dma_start(STREAM[:, n, :], quant_src(w, t + 1, n)).then_inc(S(f"stream_in{n}"), 16)

            sp.wait_ge(S("aT_ps"), 2 * NT)
            for n in range(4):
                sp.dma_start(STREAM[:, n, :], quant_src(0, 0, n)).then_inc(S(f"stream_in{n}"), 16)

            def h_moves(t, j, more=True):
                load_split(Wneigh1, t, j, 40 + t)
                quant_moves(0, t, j, more)

            steps(sp, 0, 6, h_moves)
            h_moves(6, 0)
            h_moves(7, 1, False)

            for t in range(2):
                sp.wait_ge(S(f"u_out{t}"), 16 * NT // 2)
                if t == 1:
                    sp.wait_ge(S("h_t1"), NT)
                else:
                    sp.wait_ge(S("q8_out0"), 16 * 16)
                    sp.wait_ge(S("q8_out1"), 16 * 16)
                sp.dma_start(XIN[:, t, :], rows(u_d, t)).then_inc(S(f"x_in{t}"), 16)
            steps(sp, 0, 8, lambda t, j: load_split(Wself1, t, j, 48 + t))
            sp.wait_ge(S("quantized"), 32)
            for n in range(4):
                sp.dma_start(STREAM[:, n, :], quant_src(1, 0, n)).then_inc(S(f"stream_in{n}"), 16)

            sp.wait_ge(S("z1_ps"), NT)
            sp.dma_start(S0[:, :], wq_d[0]).then_inc(S("w1q_in"), 16)
            sp.wait_ge(S("split_lo"), 56)

            def x1_moves(t, j, quant=True, more=True):
                if quant:
                    quant_moves(1, t, j, more)
                    sp.wait_ge(S("x1_t1"), t + 1)
                    sp.dma_start(XIN[:, j, :], rows(u_d, t + 2)).then_inc(S(f"x_in{j}"), 16)
                sp.wait_ge(S("x1"), t + 1)
                sp.dma_start(rows(x1_d, t), TMP[:, 1, :]).then_inc(S("x1_out"), 16)

            steps(sp, 0, 6, x1_moves)
            x1_moves(6, 0)
            x1_moves(7, 1, True, False)
            x1_moves(8, 0, False)
            x1_moves(9, 1, False)

            sp.wait_ge(S("s1_ps"), NT)
            sp.wait_ge(S("q8_out0"), 32 * 16)
            sp.wait_ge(S("q8_out1"), 32 * 16)
            sp.dma_start(S1[:, :], wq_d[1]).then_inc(S("w2q_in"), 16)
            sp.wait_ge(S("x1_out"), 16 * NT)
            for t in range(2):
                sp.dma_start(x1_in[:, t, :], rows(x1_d, t)).then_inc(S(f"x1_in{t}"), 16)

            def y_moves(t, j, more=True):
                sp.wait_ge(S("y"), t + 1)
                sp.dma_start(rows(out, t), y_out[:, j, :]).then_inc(S(f"y_out{j}"), 16)
                if more:
                    sp.dma_start(x1_in[:, j, :], rows(x1_d, t + 2)).then_inc(S(f"x1_in{j}"), 16)

            steps(sp, 0, 8, y_moves)
            for t in range(8, NT):
                y_moves(t, t % 2, False)
            for j in range(2):
                sp.wait_ge(S(f"y_out{j}"), 16 * NT // 2)

        @block.gpsimd
        def _(pool):
            nc.gpsimd.memset(ident[:, :], 0.0).then_inc(S("ident0"), 1)
            pool.wait_ge(S("ident0"), 1)
            nc.gpsimd.affine_select(out=ident[:, :], in_=ident[:, :], compare_op=ALU.not_equal, fill=1.0, base=0,
                                    pattern=[[-1, P]], channel_multiplier=1).then_inc(S("ident"), 1)
            nc.gpsimd.memset(zero[:, :], 0.0).then_inc(S("zero"), 1)
            nc.gpsimd.memset(ones[:, :], 1.0).then_inc(S("ones"), 1)
            nc.gpsimd.memset(col("magic"), MAGIC).then_inc(S("consts"), 1)
            nc.gpsimd.memset(col("eps"), EPS_LN).then_inc(S("consts"), 1)
            nc.gpsimd.iota(col("first"), [[P, NT]], base=0, channel_multiplier=0,
                           allow_small_or_imprecise_dtypes=True).then_inc(S("consts"), 1)
            nc.gpsimd.iota(col("chunk1"), [[P, 2]], base=1, channel_multiplier=1,
                           allow_small_or_imprecise_dtypes=True).then_inc(S("consts"), 1)
            nc.gpsimd.iota(col("chunk_left"), [[-P, 2]], base=2 * P, channel_multiplier=-1,
                           allow_small_or_imprecise_dtypes=True).then_inc(S("consts"), 1)
            pool.wait_ge(S("v_t"), NT)
            nc.gpsimd.memset(kvT, 0.0).then_inc(S("kvT0"), 1)
            pool.wait_ge(S("blk_v"), 4)
            nc.gpsimd.partition_all_reduce(blk[:, 80:120], blk[:, 40:80], P, RMAX).then_inc(S("blk_r"), 1)
            pool.wait_ge(S("xT_lo"), NT)
            nc.gpsimd.iota(iota, [[1, NP_]], base=0, channel_multiplier=0,
                           allow_small_or_imprecise_dtypes=True).then_inc(S("iota"), 1)

            pool.wait_ge(S("k_ps"), NT)
            nc.gpsimd.memset(qT[:, :, :, N:NP_], 0.0).then_inc(S("pad0"), 1)
            pool.wait_ge(S("stream_used"), 112)
            nc.gpsimd.memset(a_row[:, N:NP_], 0.0).then_inc(S("pad0"), 1)

            def x2_pool(t, j):
                pool.wait_ge(S("x2T"), t + 1)
                wait(pool, "f1_ps", 8 * (t - 1))
                nc.gpsimd.tensor_copy(x2_tile[:, j, :, :], x2T[:, :, tile_of(t)]).then_inc(S("x2_tile"), 1)

            pool.wait_ge(S("split_lo"), 56)
            x2_pool(0, 0)
            x2_pool(1, 1)
            steps(pool, 2, NT, x2_pool)

        @block.scalar
        def _(act):
            A = nc.scalar.activation

            def ln_std(t):
                act.wait_ge(S("ln_mv"), t + 1)
                A(col("ln_std"), mv[:, 1:2], ACT.Sqrt, bias=col("eps")).then_inc(S("ln_std"), 1)

            def ln_hi(t, j):
                act.wait_ge(S("ln_xn"), t + 1)
                A(HL[:, j, 0, :], TMP[:, 0, :], ACT.Copy, scale=X_SCALE).then_inc(S("ln_hi"), 1)

            def xT_act(t):
                act.wait_ge(S("xT_ps"), 2 * t + 1)
                alone(act)
                A(XH[:, 0, :, tile_of(t)], turned(2), ACT.Copy).then_inc(S("xT_hi"), 1)

            def norm(name, n, count):
                act.wait_ge(S("norm_ps"), count)
                A(col(name), ps[:, NORM_AT[count]:NORM_AT[count] + n], ACT.Sqrt).then_inc(S("norm"), 1)

            def split(dst, src, scale):
                A(dst, src, ACT.Copy, scale=scale).then_inc(S("split_hi"), 1)

            def split_chunk(dst, kc, slot, idx, scale):
                act.wait_ge(S(f"split_in{slot}"), 8 * (idx - KC * WQ - slot) + 16)
                alone(act)
                split(dst[:, kc, 0, :], SPLIT[:, slot, :], scale)

            def square(n, kc):
                if n == 0:
                    act.wait_ge(S(f"wk_in{kc}"), 16)
                else:
                    act.wait_ge(S(f"wv_in{kc // 2}"), 32)
                wait(act, "squared", 8 * n + kc - 3)
                A(kv[:, 1, kc % 4, :], Wv_raw(kc) if n else raw[:, kc, :], ACT.Square,
                  accum_out=NPW[:, n, kc:kc + 1]).then_inc(S("squared"), 1)

            def k_hi(t, j):
                act.wait_ge(S("k_t"), t + 1)
                A(kv[:, j, 0, :], TMP[:, 1, :], ACT.Relu).then_inc(S("k_hi"), 1)

            def v_hi(t, j):
                act.wait_ge(S("v_t"), t + 1)
                A(kv[:, j, 2, :], TMP[:, 1, :], ACT.Copy).then_inc(S("v_hi"), 1)

            act.wait_ge(S("consts"), 5)
            ln_std(0)
            square(0, 0)
            ln_hi(0, 0)
            square(0, 1)
            square(0, 2)
            xT_act(0)
            for kc in range(3, KC):
                square(0, kc)
            ln_std(1)
            norm("norm_kv0", 1, 1)
            act.wait_ge(S("scales"), 1)
            for kc in range(KC):
                split(Wk_s[:, kc, 0, :], raw[:, kc, :], at("s", WK))
                if kc == 3:
                    ln_hi(1, 1)
            xT_act(1)
            for kc in range(KC):
                square(1, kc)
            ln_std(2)
            k_hi(0, 0)
            norm("norm_kv1", 1, 2)
            act.wait_ge(S("scales"), 2)
            for kc in range(KC):
                split(Wv_s[:, kc, 0, :], Wv_raw(kc), at("s", WV))
                if kc == 1:
                    ln_hi(2, 0)
            v_hi(0, 0)

            def kv_act(t, j, ln=True, norms=True, split_too=False):
                if norms:
                    xT_act(t + 1)
                k_hi(t, j)
                if split_too:
                    for n in range(2):
                        kc = 2 * (t - 4) + n
                        split_chunk(Wq_s, kc, n, KC * WQ + kc, at("s", WQ))
                if norms:
                    for n in range(NORMS + KV_MEANS):
                        if ln and n == 2:
                            ln_std(t + 2)
                        if ln and n == 3:
                            ln_hi(t + 2, j)
                        act.wait_ge(S(f"stream_in{n % 4}"), 32 * (t - 1) + 16 * (n // 4) + 16)
                        alone(act)
                        if n < NORMS:
                            total = NPW_all[:, bass.ds(WQ * KC + NORMS * (t - 1) + n, 1)]
                        else:
                            total = MW_all[:, bass.ds(KV_MEANS * (t - 1) + n - NORMS, 1)]
                        A(STREAM[:, n % 4, :], STREAM[:, n % 4, :], ACT.Square if n < NORMS else ACT.Abs,
                          accum_out=total).then_inc(S("stream_used"), 1)
                v_hi(t, j)

            steps(act, 1, 3, lambda t, j: kv_act(t, 1 - j))
            kv_act(3, 1)
            norm("norm_q", 2, 3)
            act.wait_ge(S("scales"), 3)
            steps(act, 4, 8, lambda t, j: kv_act(t, j, split_too=True))
            kv_act(8, 0, ln=False)
            norm("norm5", 5, 4)
            kv_act(9, 1, ln=False, norms=False)

            def q_hi(m, j):
                act.wait_ge(S("q_t"), m + 1)
                alone(act)
                A(qT[:, 0, m, 0:N], q_t[:, j, 0:N], ACT.Relu).then_inc(S("q_hi"), 1)

            def add_up(c, slot, count):
                act.wait_ge(S(f"stream_in{slot}"), count)
                alone(act)
                A(STREAM[:, slot, :], STREAM[:, slot, :], ACT.Abs,
                  accum_out=MW_all[:, bass.ds(c, 1)]).then_inc(S("stream_used"), 1)

            def q_means(m):
                for n in range(Q_MEANS):
                    add_up(Q_FIRST + Q_MEANS * m + n, n, 16 * 16 + 16 * m + 16)

            def u_means(t, j):
                for n in range(U_MEANS):
                    add_up(U_FIRST + U_MEANS * t + n, U_MEANS * j + n, (16 + 8) * 16 + 8 * (t - j) + 16)

            def m_hi(p, bank):
                act.wait_ge(S("m_ps"), p + 1)
                alone(act)
                A(M_s[:, p, 0, :], banks(bank), ACT.Copy, scale=col("a_m")).then_inc(S("m_hi"), 1)

            def q_act(m, j):
                q_hi(m, j)
                m_hi(m - 3, 6)
                q_means(m)

            for m in range(3):
                q_hi(m, m % 2)
                if m == 0:
                    act.wait_ge(S("kvT"), 16)
                    A(banks(6), kvT, ACT.Square, accum_out=col("kv_sq")).then_inc(S("kv_sq"), 1)
                if m == 2:
                    norm("norm_m", 1, 5)
                q_means(m)
            act.wait_ge(S("a_m"), 1)
            q_act(3, 1)
            steps(act, 4, 6, q_act)
            q_act(6, 0)
            q_hi(7, 1)
            m_hi(4, 6)
            for p in range(5, KC):
                m_hi(p, M_BANK[p])
            q_means(7)

            act.wait_ge(S("scales"), 4)

            def u_act(t, j):
                split_chunk(weight(S0), t, j, 24 + t, at("s", WN0))
                u_means(t, j)

            steps(act, 0, 8, u_act)

            def z_act(name, t, bank, scale):
                act.wait_ge(S(name + "_ps"), t + 1)
                alone(act)
                A(Z[:, 0, t, :], banks(bank), ACT.Copy, scale=scale).then_inc(S(name + "_hi"), 1)

            def count_act(t, j, split_too=True):
                act.wait_ge(S("a_ps"), t + 1)
                wait(act, "aT_ps", 2 * t)
                alone(act)
                A(a_row[:, 0:N], banks(0, cut=N), ACT.Copy, accum_out=at("deg", t)).then_inc(S("a_row"), 1)
                if split_too:
                    split_chunk(weight(S1), t, j, 32 + t, at("s", WS0))
                act.wait_ge(S("aT_ps"), 2 * t + 1)
                alone(act)
                A(ATv[:, 0:8, tile_of(t)], turned(3), ACT.Copy).then_inc(S("aT_hi"), 1)
                act.wait_ge(S("aT_ps"), 2 * t + 2)
                alone(act)
                A(ATv[:, 8:NT, tile_of(t)], turned(3)[:, 0:NT - 8, :], ACT.Copy).then_inc(S("aT_lo"), 1)
                z_act("z0", t, 4 + 2 * j, Z0_SCALE)

            for j in range(2):
                act.wait_ge(S(f"u_out{j}"), 16 * NT // 2)
            act.wait_ge(S("u_ps"), NT)
            steps(act, 0, 8, count_act)
            count_act(8, 0, False)
            count_act(9, 1, False)

            def hT_act(t):
                act.wait_ge(S("hT_ps"), 2 * t + 1)
                alone(act)
                A(XH[:, 0, :, tile_of(t)], turned(6), ACT.Copy).then_inc(S("hT_hi"), 1)

            def h_act(t, j, split_too=True, turn=True):
                if split_too:
                    split_chunk(weight(S0), t, j, 40 + t, at("s", WN1))
                if turn:
                    hT_act(t - 1)
                act.wait_ge(S("h_t2"), t + 1)
                A(HL[:, j, 0, :], TMP[:, 1, :], ACT.Relu).then_inc(S("h_hi"), 1)
                wait(act, "h_sq", t)
                act.wait_ge(S("h_hi"), t + 1)
                alone(act)
                A(banks(4), HL[:, j, 0, :], ACT.Square, accum_out=at("h_sq", t)).then_inc(S("h_sq"), 1)

            h_act(0, 0, turn=False)
            h_act(1, 1)
            steps(act, 2, 8, h_act)
            h_act(8, 0, False)
            h_act(9, 1, False)
            hT_act(9)

            norm("norm_h", 1, 6)
            act.wait_ge(S("f_z1"), 1)

            def z1_act(t, j):
                split_chunk(weight(S1), t, j, 48 + t, at("s", WS1))
                z_act("z1", t, 4 * j, col("f_z1"))

            steps(act, 0, 8, z1_act)
            for t in range(8, NT):
                z_act("z1", t, 4 * (t % 2), col("f_z1"))

            def y_std(t):
                act.wait_ge(S("y_mv"), t + 1)
                A(col("y_std"), mv[:, 1:2], ACT.Sqrt, bias=col("eps")).then_inc(S("y_std"), 1)

            def y_round(t):
                act.wait_ge(S("y_sc"), t + 1)
                A(x2n, x2n, ACT.Identity, bias=col("magic"), scale=col("y_sc")).then_inc(S("r_magic"), 1)

            def x1_act(t, j):
                y_std(t)
                y_round(t)

            steps(act, 0, 8, x1_act)
            x1_act(8, 0)

            def gelu(t, slot, part=range(8)):
                for n in part:
                    act.wait_ge(S("f1_ps"), 8 * t + n + 1)
                    alone(act)
                    A(hid[:, slot, n * BANK:(n + 1) * BANK], banks(n % 4, 1), ACT.Gelu,
                      scale=at("dq1", t)).then_inc(S("gelu"), 1)

            def hid_round(t, slot):
                act.wait_ge(S("g_sc"), t + 1)
                for n in range(4):
                    piece = hid[:, slot, n * D:(n + 1) * D]
                    A(piece, piece, ACT.Identity, bias=col("magic"), scale=col("g_sc")).then_inc(S("g_magic"), 1)

            def hidT_act(t, slot, n):
                act.wait_ge(S("gT_ps"), 4 * t + n + 1)
                alone(act)
                A(hid_T[:, slot, 8 * n:8 * n + 8, :], turned(6), ACT.Copy).then_inc(S("gT_hi"), 1)

            def ffn_act(t, j, more=True, ahead=0):
                if ahead:
                    gelu(t + 1, 1 - j, range(ahead))
                hid_round(t, j)
                if more:
                    gelu(t + 1, 1 - j, range(ahead, 7))
                hidT_act(t, j, 0)
                if more:
                    gelu(t + 1, 1 - j, range(7, 8))
                hidT_act(t, j, 2)

            y_std(9)
            gelu(0, 0, range(2))
            y_round(9)
            gelu(0, 0, range(2, 8))
            ffn_act(0, 0, ahead=4)
            ffn_act(1, 1)
            steps(act, 2, 8, ffn_act)
            ffn_act(8, 0)
            ffn_act(9, 1, False)

        @block.vector
        def _(dve):
            V = nc.vector
            small = [0]

            def link(ins):
                small[0] += 1
                ins.then_inc(S("cols"), 1)
                dve.wait_ge(S("cols"), small[0])

            def pow2(dst, a):
                link(V.tensor_scalar(dst, a, TINY, None, ALU.max))
                link(V.tensor_scalar(dst.bitcast(I32), dst.bitcast(I32), POW2_MASK, None, ALU.bitwise_and))

            def ratio(dst, a, num):
                link(V.reciprocal(dst, a))
                link(V.tensor_scalar(dst, dst, num, None, ALU.mult))

            def times(dst, a, b, c=1.0):
                link(V.tensor_scalar(dst, a, b, c, ALU.mult, ALU.mult))

            def range_scale(dst, a):
                pow2(dst, a)
                ratio(dst, dst, W_SCALE)

            def ln_stats(t, j):
                dve.wait_ge(S(f"x_in{j}"), 8 * (t - j) + 16)
                wait(dve, "ln_lo", t)
                for n in range(2):
                    V.bn_stats(st[:, 6 * n:6 * n + 6], XIN[:, j, n * 512:(n + 1) * 512]).then_inc(S("ln_stats"), 1)
                dve.wait_ge(S("ln_stats"), 2 * t + 2)
                alone(dve)
                V.bn_aggr(mv[:, :], st[:, :]).then_inc(S("ln_mv"), 1)

            def ln_xn(t, j):
                dve.wait_ge(S("ln_std"), t + 1)
                V.reciprocal(col("ln_rstd"), col("ln_std")).then_inc(S("ln_rstd"), 1)
                dve.wait_ge(S("ln_rstd"), t + 1)
                V.tensor_scalar(TMP[:, 0, :], XIN[:, j, :], mv[:, 0:1], col("ln_rstd"),
                                ALU.subtract, ALU.mult).then_inc(S("ln_xn"), 1)

            def ln_lo(t, j):
                dve.wait_ge(S("ln_hi"), t + 1)
                V.scalar_tensor_tensor(HL[:, j, 1, :], TMP[:, 0, :], X_SCALE, HL[:, j, 0, :],
                                       ALU.mult, ALU.subtract).then_inc(S("ln_lo"), 1)

            def xT_dve(t):
                dve.wait_ge(S("xT_ps"), 2 * t + 2)
                V.tensor_copy(XH[:, 1, :, tile_of(t)], turned(3)).then_inc(S("xT_lo"), 1)

            def split(dst, src, scale, idx):
                dve.wait_ge(S("split_hi"), idx + 1)
                V.scalar_tensor_tensor(dst[:, 1, :], src, scale, dst[:, 0, :],
                                       ALU.mult, ALU.subtract).then_inc(S("split_lo"), 1)

            def split_chunk(dst, kc, slot, idx, scale):
                dve.wait_ge(S("split_hi"), idx + 1)
                V.scalar_tensor_tensor(dst[:, kc, 1, :], SPLIT[:, slot, :], scale, dst[:, kc, 0, :],
                                       ALU.mult, ALU.subtract).then_inc(S("split_lo"), 1)

            def weight_scale(n, w):
                dve.wait_ge(S("norm"), n + 1)
                pow2(at("p", w), col("norm_kv" + str(n)))
                link(V.reciprocal(at("s", w), at("p", w)))
                V.tensor_scalar(at("s", w), at("s", w), W_SCALE, None, ALU.mult).then_inc(S("scales"), 1)
                dve.wait_ge(S("scales"), n + 1)

            def bias_max(n):
                dve.wait_ge(S("bk_in" if n == 0 else "bv_in"), 16)
                link(V.tensor_reduce(col("a_kv" + str(n)), b_kv[:, n, :], AXX, ALU.max, apply_absolute_value=True))

            def kv_scale(n, w):
                a, c = col("a_kv" + str(n)), col("c_kv" + str(n))
                link(V.scalar_tensor_tensor(a, at("p", w), 2.0 ** 6, a, ALU.mult, ALU.add))
                range_scale(a, a)
                link(V.tensor_scalar(b_kv[:, n, :], b_kv[:, n, :], a, None, ALU.mult))
                times(c, at("p", w), a, 1.0 / XW)

            def square_sum(n, w):
                dve.wait_ge(S("squared"), 8 * (n + 1))
                V.tensor_reduce(col("sq" + str(n)), NPW[:, w, :], AXX, ALU.add).then_inc(S("sq"), 1)

            def k_t(t):
                dve.wait_ge(S("k_ps"), t + 1)
                wait(dve, "v_lo", t)
                V.scalar_tensor_tensor(TMP[:, 1, :], banks(0), col("c_kv0"), b_kv[:, 0, :],
                                       ALU.mult, ALU.add).then_inc(S("k_t"), 1)

            def k_lo(t, j):
                dve.wait_ge(S("k_hi"), t + 1)
                V.scalar_tensor_tensor(kv[:, j, 1, :], TMP[:, 1, :], 0.0, kv[:, j, 0, :],
                                       ALU.max, ALU.subtract).then_inc(S("k_lo"), 1)

            def v_dve(t, j):
                dve.wait_ge(S("v_ps"), t + 1)
                dve.wait_ge(S("k_lo"), t + 1)
                V.scalar_tensor_tensor(TMP[:, 1, :], banks(4), col("c_kv1"), b_kv[:, 1, :],
                                       ALU.mult, ALU.add).then_inc(S("v_t"), 1)
                dve.wait_ge(S("v_hi"), t + 1)
                V.tensor_tensor(kv[:, j, 3, :], TMP[:, 1, :], kv[:, j, 2, :],
                                ALU.subtract).then_inc(S("v_lo"), 1)

            dve.wait_ge(S("consts"), 5)
            ln_stats(0, 0)
            ln_xn(0, 0)
            ln_lo(0, 0)
            xT_dve(0)
            ln_stats(1, 1)
            square_sum(0, WK)
            ln_xn(1, 1)
            weight_scale(0, WK)
            for kc in range(KC):
                split(Wk_s[:, kc, :, :], raw[:, kc, :], at("s", WK), kc)
                if kc == 3:
                    ln_lo(1, 1)
            bias_max(0)
            xT_dve(1)
            kv_scale(0, WK)
            k_t(0)
            ln_stats(2, 0)
            bias_max(1)
            square_sum(1, WV)
            ln_xn(2, 0)
            k_lo(0, 0)
            weight_scale(1, WV)
            for kc in range(KC):
                split(Wv_s[:, kc, :, :], Wv_raw(kc), at("s", WV), KC + kc)
                if kc == 1:
                    kv_scale(1, WV)
                if kc == 2:
                    ln_lo(2, 0)
            v_dve(0, 0)

            def kv_dve(t, j, ln=True, turn=True, split_too=False):
                if turn:
                    xT_dve(t + 1)
                k_t(t)
                k_lo(t, j)
                if split_too:
                    for n in range(2):
                        kc = 2 * (t - 4) + n
                        split_chunk(Wq_s, kc, n, KC * WQ + kc, at("s", WQ))
                if ln:
                    ln_stats(t + 2, j)
                    ln_xn(t + 2, j)
                    ln_lo(t + 2, j)
                v_dve(t, j)

            def other_scales(count, ws, norms):
                dve.wait_ge(S("norm"), count)
                pw, sw = col("p")[:, ws], col("s")[:, ws]
                pow2(pw, norms)
                link(V.reciprocal(sw, pw))
                V.tensor_scalar(sw, sw, W_SCALE, None, ALU.mult).then_inc(S("scales"), 1)
                dve.wait_ge(S("scales"), count)

            steps(dve, 1, 3, lambda t, j: kv_dve(t, 1 - j))
            dve.wait_ge(S("bq_in"), 16)
            link(V.tensor_tensor(col("bq2"), col("bq"), col("bq"), ALU.mult))
            V.tensor_reduce(col("sq_q")[:, 1:2], col("bq2"), AXX, ALU.add).then_inc(S("sq"), 1)
            dve.wait_ge(S("stream_used"), KC + KV_MEANS)
            V.tensor_reduce(col("sq_q")[:, 0:1], NPW[:, WQ, :], AXX, ALU.add).then_inc(S("sq"), 1)
            kv_dve(3, 1)
            other_scales(3, slice(WQ, WQ + 1), col("norm_q")[:, 0:1])
            link(V.scalar_tensor_tensor(col("a_q"), at("p", WQ), 2.0 ** 6, col("norm_q")[:, 1:2],
                                        ALU.mult, ALU.add))
            range_scale(col("a_q"), col("a_q"))
            times(col("c_q"), at("p", WQ), col("a_q"), 1.0 / XW)
            V.tensor_scalar(col("bqs"), col("bq"), col("a_q"), None, ALU.mult).then_inc(S("c_q"), 1)
            dve.wait_ge(S("c_q"), 1)
            steps(dve, 4, 8, lambda t, j: kv_dve(t, j, split_too=True))
            kv_dve(8, 0, ln=False)
            dve.wait_ge(S("stream_used"), 8 * (NORMS + KV_MEANS))
            V.tensor_reduce(col("sq5"), NPW[:, WO:, :], AXX, ALU.add).then_inc(S("sq"), 1)
            kv_dve(9, 1, ln=False, turn=False)
            other_scales(4, slice(WO, WS1 + 1), col("norm5"))

            def q_dve(m, j):
                dve.wait_ge(S("q_ps"), m + 1)
                wait(dve, "q_lo", m - 1)
                V.tensor_scalar(q_t[:, j, 0:N], banks(3 * j, cut=N), col("c_q"), at("bqs", m),
                                ALU.mult, ALU.add).then_inc(S("q_t"), 1)
                dve.wait_ge(S("q_hi"), m + 1)
                V.scalar_tensor_tensor(qT[:, 1, m, 0:N], q_t[:, j, 0:N], 0.0, qT[:, 0, m, 0:N],
                                       ALU.max, ALU.subtract).then_inc(S("q_lo"), 1)

            q_dve(0, 0)
            dve.wait_ge(S("kv_ps"), NT)
            dve.wait_ge(S("kvT0"), 1)
            for p in range(KC):
                for h in range(2):
                    r = slice(DH * h, DH * h + DH)
                    c = P * p + DH * h
                    V.tensor_copy(kvT[r, c:c + DH], ps[r, 6 * BANK + c:6 * BANK + c + DH]).then_inc(S("kvT"), 1)
            q_dve(1, 1)

            dve.wait_ge(S("edges_in"), 48)
            V.tensor_copy(srcf[:, :], edges[:, 0, :]).then_inc(S("edges_f"), 1)
            V.tensor_copy(dstf[:, :], edges[:, 1, :]).then_inc(S("edges_f"), 1)
            link(V.tensor_copy(d_flt, d_int))
            link(V.tensor_reduce(blk[:, 0:2], d_flt, AXX, ALU.min))
            link(V.tensor_reduce(blk[:, 2:4], d_flt, AXX, ALU.max))
            link(V.tensor_scalar(blk[:, 0:2], blk[:, 0:2], -(P - 1.0), None, ALU.add))
            for g in range(2):
                a, b = blk[:, 10:20], blk[:, 20:30]
                link(V.tensor_scalar(a, col("first"), blk[:, 2 + g:3 + g], None, ALU.is_le))
                link(V.tensor_scalar(b, col("first"), blk[:, g:g + 1], None, ALU.is_ge))
                link(V.tensor_tensor(a, a, b, ALU.mult))
                V.tensor_scalar(blk[:, 40 + 10 * g:50 + 10 * g], a, col("chunk_left")[:, g:g + 1], None,
                                ALU.mult).then_inc(S("blk_v"), 1)
                V.tensor_scalar(blk[:, 60 + 10 * g:70 + 10 * g], a, col("chunk1")[:, g:g + 1], None,
                                ALU.mult).then_inc(S("blk_v"), 1)
                dve.wait_ge(S("blk_v"), 2 * g + 2)
            dve.wait_ge(S("blk_r"), 1)
            lo, hi = blk[:, 0:10], blk[:, 10:20]
            link(V.tensor_tensor(lo, blk[:, 80:90], blk[:, 90:100], ALU.max))
            link(V.tensor_scalar(lo, lo, -1.0, 2.0 * P, ALU.mult, ALU.add))
            link(V.tensor_scalar(lo, lo, EC - 1.0, None, ALU.min))
            link(V.tensor_tensor(hi, blk[:, 100:110], blk[:, 110:120], ALU.max))
            link(V.tensor_scalar(blk[:, 20:30], lo, QUAD + 1.0, None, ALU.add))
            link(V.tensor_tensor(hi, hi, blk[:, 20:30], ALU.max))
            V.tensor_copy(bnd[:, 0, :], lo).then_inc(S("bounds"), 1)
            V.tensor_copy(bnd[:, 1, :], hi).then_inc(S("bounds"), 1)

            q_dve(2, 0)
            dve.wait_ge(S("norm"), 5)
            times(col("a_m"), col("norm_m"), col("norm5")[:, 0:1])
            pow2(col("a_m"), col("a_m"))
            link(V.reciprocal(col("a_m"), col("a_m")))
            V.tensor_scalar(col("a_m"), col("a_m"), W_SCALE, None, ALU.mult).then_inc(S("a_m"), 1)
            dve.wait_ge(S("a_m"), 1)
            c = col("c_u")
            link(V.reciprocal(c, col("a_q")))
            for name in ("a_kv0", "a_kv1", "a_m"):
                link(V.reciprocal(col("inv"), col(name)))
                times(c, c, col("inv"))
            times(c, c, 1.0 / (N * DH))

            def m_dve(p, bank):
                dve.wait_ge(S("m_hi"), p + 1)
                V.scalar_tensor_tensor(M_s[:, p, 1, :], banks(bank), col("a_m"), M_s[:, p, 0, :],
                                       ALU.mult, ALU.subtract).then_inc(S("m_lo"), 1)

            q_dve(3, 1)
            m_dve(0, 6)

            def qm_dve(m, j):
                q_dve(m, j)
                m_dve(m - 3, 6)

            steps(dve, 4, 8, qm_dve)
            for p in range(5, KC):
                m_dve(p, M_BANK[p])
            dve.wait_ge(S("b_out_in"), 32)
            link(V.tensor_tensor(b_out, b_out, TMP[:, 1, :], ALU.add))

            def u_dve(t, j, split_too=True, first=False):
                dve.wait_ge(S("u_ps"), t + 1)
                dve.wait_ge(S(f"x_in{j}"), 80 + 8 * (t - j) + 16)
                wait(dve, "u", t)
                V.scalar_tensor_tensor(TMP[:, 0, :], banks(4 * j), c, XIN[:, j, :],
                                       ALU.mult, ALU.add).then_inc(S("u_t"), 1)
                dve.wait_ge(S("u_t"), t + 1)
                if not first:
                    dve.wait_ge(S(f"u_out{j}"), 8 * (t - j))
                V.tensor_tensor(u_out[:, j, :], TMP[:, 0, :], b_out, ALU.add).then_inc(S("u"), 1)
                if split_too:
                    split_chunk(weight(S0), t, j, 24 + t, at("s", WN0))

            u_dve(0, 0, first=True)
            u_dve(1, 1, first=True)
            steps(dve, 2, 8, u_dve)
            u_dve(8, 0, False)
            dve.wait_ge(S("stream_used"), 112)
            V.tensor_reduce(col("w_sum"), MW[:, :, :], AXX, ALU.add).then_inc(S("sq"), 1)

            made = dve.alloc_register("made")
            dve.reg_mov(made, 0)

            def hots(b, first, reuse=True):
                n = dve.snap(made) if reuse else 0
                for j in range(QUAD):
                    if reuse:
                        dve.wait_ge(S("hot_free"), n + (j + 1))
                        alone(dve)
                    V.tensor_scalar(hot_src[:, j, 0:N], iota[:, 0:N], srcf[:, bass.ds(first + j, 1)], None,
                                    ALU.is_equal).then_inc(S("hot_src"), 1)
                    V.tensor_scalar(hot_dst[:, j, :], iota[:, tile_of(b)], dstf[:, bass.ds(first + j, 1)], None,
                                    ALU.is_equal).then_inc(S("hot_dst"), 1)
                if reuse:
                    dve.reg_add(made, made, QUAD)

            def bound(i, b, **least_and_most):
                return dve.value_load(bnd[0:1, i, bass.ds(b, 1)], **least_and_most)

            def first_hots(b, reuse=True):
                hots(b, bound(0, b, min_val=0, max_val=EC - 1), reuse)

            def z_dve(name, t, bank, scale):
                dve.wait_ge(S(name + "_hi"), t + 1)
                V.scalar_tensor_tensor(Z[:, 1, t, :], banks(bank), scale, Z[:, 0, t, :],
                                       ALU.mult, ALU.subtract).then_inc(S(name + "_lo"), 1)

            def count_dve(t, j, split_too=True, more=True, z=True):
                first = bound(0, t, min_val=0, max_val=EC - 1)
                last = bound(1, t, min_val=QUAD + 1, max_val=EC + QUAD)
                with dve.Fori(first + QUAD, last, QUAD) as c_:
                    hots(t, c_)
                if z:
                    z_dve("z0", t - 1, 6 - 2 * j, Z0_SCALE)
                if split_too:
                    split_chunk(weight(S1), t, j, 32 + t, at("s", WS0))
                if more:
                    first_hots(t + 1)

            dve.wait_ge(S("bounds"), 2)
            dve.wait_ge(S("edges_f"), 2)
            dve.wait_ge(S("iota"), 1)
            first_hots(0, reuse=False)
            u_dve(9, 1, False)
            count_dve(0, 0, z=False)
            count_dve(1, 1)
            dve.wait_ge(S("mean_ps"), 1)
            sw = col("w_mean")
            link(V.tensor_scalar(sw, ps[:, MEAN_AT:MEAN_AT + 2], 1.0 / (HID * D), EPS_Q, ALU.mult, ALU.max))
            link(V.tensor_scalar(col("thr"), sw, 0.5, None, ALU.mult))
            link(V.tensor_scalar(col("nthr"), sw, -0.5, None, ALU.mult))
            link(V.tensor_scalar(col("nsw"), sw, -1.0 / 127.0, None, ALU.mult))
            steps(dve, 2, 8, count_dve)
            count_dve(8, 0, False)
            count_dve(9, 1, False, more=False)
            z_dve("z0", 9, 6, Z0_SCALE)

            dve.wait_ge(S("a_row"), NT)
            deg = col("deg")
            link(V.tensor_scalar(deg, deg, 1.0, None, ALU.max))
            link(V.reciprocal(deg, deg))
            dve.wait_ge(S("b0_in"), 16)
            b0s = XIN[:, 1, :]
            a = col("a_h")
            link(V.tensor_reduce(a, b0s, AXX, ALU.max, apply_absolute_value=True))
            link(V.scalar_tensor_tensor(a, at("p", WS0), 2.0 ** 6, a, ALU.mult, ALU.add))
            link(V.scalar_tensor_tensor(a, at("p", WN0), 2.0 ** 6, a, ALU.mult, ALU.add))
            range_scale(a, a)
            link(V.tensor_scalar(b0s, b0s, a, None, ALU.mult))
            times(col("c_h"), at("p", WS0), a, 1.0 / XW)
            times(col("tmp"), at("p", WN0), a, 1.0 / (XW * Z0_SCALE))
            times(col("deg_h"), deg, col("tmp"))

            def quantize(w, t, n, first=False):
                q8, above = q8_of[w]
                dve.wait_ge(S(f"stream_in{n}"), 28 * 16 + 128 * w + 16 * t + 16)
                wait(dve, "quantized", 32 * w + 4 * t + n)
                alone(dve)
                V.tensor_scalar(above, STREAM[:, n, :], col("thr")[:, w:w + 1], None,
                                ALU.is_gt, saturate=False).then_inc(S("above"), 1)
                dve.wait_ge(S("above"), 32 * w + 4 * t + n + 1)
                if not (first and n < 2):
                    dve.wait_ge(S(f"q8_out{n % 2}"), 256 * w + 32 * t + 16 * (n // 2))
                alone(dve)
                V.scalar_tensor_tensor(q8[:, n % 2, :], STREAM[:, n, :], col("nthr")[:, w:w + 1], above,
                                       ALU.is_lt, ALU.subtract, saturate=False).then_inc(S("quantized"), 1)

            def hT_dve(t):
                dve.wait_ge(S("hT_ps"), 2 * t + 2)
                V.tensor_copy(XH[:, 1, :, tile_of(t)], turned(7)).then_inc(S("hT_lo"), 1)

            def h_dve(t, j, quant=True, turn=True, first=False, bank=0):
                if quant:
                    split_chunk(weight(S0), t, j, 40 + t, at("s", WN1))
                    for n in range(2):
                        quantize(0, t, n, first)
                if turn:
                    hT_dve(t - 1)
                dve.wait_ge(S("g0_ps"), t + 1)
                wait(dve, "h_lo", t)
                V.scalar_tensor_tensor(TMP[:, 0, :], banks(bank), at("deg_h", t), b0s,
                                       ALU.mult, ALU.add).then_inc(S("h_t1"), 1)
                if quant:
                    for n in range(2, 4):
                        quantize(0, t, n)
                dve.wait_ge(S("s0_ps"), t + 1)
                dve.wait_ge(S("h_t1"), t + 1)
                V.scalar_tensor_tensor(TMP[:, 1, :], banks(2), col("c_h"), TMP[:, 0, :],
                                       ALU.mult, ALU.add).then_inc(S("h_t2"), 1)
                dve.wait_ge(S("h_hi"), t + 1)
                V.scalar_tensor_tensor(HL[:, j, 1, :], TMP[:, 1, :], 0.0, HL[:, j, 0, :],
                                       ALU.max, ALU.subtract).then_inc(S("h_lo"), 1)

            h_dve(0, 0, turn=False, first=True, bank=4)
            h_dve(1, 1)
            steps(dve, 2, 8, h_dve)
            h_dve(8, 0, False)
            h_dve(9, 1, False)
            hT_dve(9)

            dve.wait_ge(S("h_sq"), NT)
            V.tensor_reduce(col("sq_h"), col("h_sq"), AXX, ALU.add).then_inc(S("sq"), 1)
            dve.wait_ge(S("norm"), 6)
            f = col("f_z1")
            pow2(f, col("norm_h"))
            link(V.reciprocal(f, f))
            V.tensor_scalar(f, f, 0.5, None, ALU.mult).then_inc(S("f_z1"), 1)
            dve.wait_ge(S("f_z1"), 1)
            link(V.reciprocal(col("inv"), col("a_h")))
            times(col("c_x"), at("p", WS1), col("inv"), 1.0 / W_SCALE)
            times(col("tmp"), at("p", WN1), col("inv"), 1.0 / W_SCALE)
            link(V.reciprocal(col("inv"), f))
            times(col("tmp"), col("tmp"), col("inv"))
            times(col("deg_x"), deg, col("tmp"))

            def z1_dve(t, j):
                split_chunk(weight(S1), t, j, 48 + t, at("s", WS1))
                z_dve("z1", t, 4 * j, f)

            steps(dve, 0, 8, z1_dve)
            for t in range(8, NT):
                z_dve("z1", t, 4 * (t % 2), f)

            def x2T_dve(t):
                dve.wait_ge(S("x2T_ps"), t + 1)
                V.tensor_copy(x2T[:, :, tile_of(t)], turned(6)).then_inc(S("x2T"), 1)

            def x1_dve(t, j, quant=True, turn=True, first=False, bank=0):
                if first:
                    for n in range(4):
                        quantize(1, t, n)
                dve.wait_ge(S("g1_ps"), t + 1)
                dve.wait_ge(S(f"x_in{j}"), 160 + 8 * (t - j) + 16)
                wait(dve, "r", t)
                V.scalar_tensor_tensor(TMP[:, 0, :], banks(bank), at("deg_x", t), XIN[:, j, :],
                                       ALU.mult, ALU.add).then_inc(S("x1_t1"), 1)
                if turn:
                    x2T_dve(t - 1)
                if quant and not first:
                    for n in range(4):
                        quantize(1, t, n)
                dve.wait_ge(S("s1_ps"), t + 1)
                dve.wait_ge(S("x1_t1"), t + 1)
                if not first:
                    dve.wait_ge(S("x1_out"), 16 * t)
                V.scalar_tensor_tensor(TMP[:, 1, :], banks(2), col("c_x"), TMP[:, 0, :],
                                       ALU.mult, ALU.add).then_inc(S("x1"), 1)
                dve.wait_ge(S("x1"), t + 1)
                for n in range(2):
                    V.bn_stats(st[:, 6 * n:6 * n + 6], TMP[:, 1, n * 512:(n + 1) * 512]).then_inc(S("y_stats"), 1)
                dve.wait_ge(S("y_stats"), 2 * t + 2)
                alone(dve)
                V.bn_aggr(mv[:, :], st[:, :]).then_inc(S("y_mv"), 1)
                dve.wait_ge(S("y_std"), t + 1)
                V.reciprocal(col("y_rstd"), col("y_std")).then_inc(S("y_rstd"), 1)
                dve.wait_ge(S("y_rstd"), t + 1)
                V.tensor_scalar(x2n, TMP[:, 1, :], mv[:, 0:1], col("y_rstd"),
                                ALU.subtract, ALU.mult).then_inc(S("x2n"), 1)
                dve.wait_ge(S("x2n"), t + 1)
                V.tensor_reduce(col("y_max"), x2n, AXX, ALU.max, apply_absolute_value=True).then_inc(S("y_max"), 1)
                dve.wait_ge(S("y_max"), t + 1)
                V.tensor_scalar(col("y_clip"), col("y_max"), EPS_Q, None, ALU.max).then_inc(S("y_clip"), 1)
                dve.wait_ge(S("y_clip"), t + 1)
                V.tensor_scalar(at("dq1", t), col("y_clip"), col("nsw")[:, 0:1], None,
                                ALU.mult).then_inc(S("dq1"), 1)
                V.reciprocal(col("y_inv"), col("y_clip")).then_inc(S("y_inv"), 1)
                dve.wait_ge(S("y_inv"), t + 1)
                V.tensor_scalar(col("y_sc"), col("y_inv"), 127.0, None, ALU.mult).then_inc(S("y_sc"), 1)
                dve.wait_ge(S("r_magic"), t + 1)
                V.tensor_scalar(r_rows[:, j, :], x2n, -MAGIC, None, ALU.add).then_inc(S("r"), 1)

            x1_dve(0, 0, turn=False, first=True, bank=4)
            x1_dve(1, 1)
            steps(dve, 2, 8, x1_dve)
            x1_dve(8, 0, False)
            x1_dve(9, 1, False)
            x2T_dve(9)

            def hid_max(t, slot, part=range(4)):
                for n in part:
                    dve.wait_ge(S("gelu"), 8 * t + 2 * n + 2)
                    V.tensor_reduce(AM[:, n:n + 1], hid[:, slot, n * D:(n + 1) * D], AXX, ALU.max,
                                    apply_absolute_value=True).then_inc(S("g_part"), 1)

            def hid_scale(t, slot):
                wait(dve, "g_sc", t)
                wait(dve, "y", t - 1)
                dve.wait_ge(S("g_part"), 4 * t + 4)
                V.tensor_reduce(col("g_max"), AM[:, :], AXX, ALU.max).then_inc(S("g_max"), 1)
                dve.wait_ge(S("g_max"), t + 1)
                V.tensor_scalar(col("g_clip"), col("g_max"), EPS_Q, None, ALU.max).then_inc(S("g_clip"), 1)
                dve.wait_ge(S("g_clip"), t + 1)
                V.tensor_scalar(at("dq2", slot), col("g_clip"), col("nsw")[:, 1:2], None,
                                ALU.mult).then_inc(S("dq2"), 1)
                V.reciprocal(col("g_inv"), col("g_clip")).then_inc(S("g_inv"), 1)
                dve.wait_ge(S("g_inv"), t + 1)
                V.tensor_scalar(col("g_sc"), col("g_inv"), 127.0, None, ALU.mult).then_inc(S("g_sc"), 1)

            def y_dve(t, j, first=False):
                dve.wait_ge(S("f2_ps"), t + 1)
                dve.wait_ge(S(f"x1_in{j}"), 8 * (t - j) + 16)
                dve.wait_ge(S("dq2"), t + 1)
                if not first:
                    dve.wait_ge(S(f"y_out{j}"), 8 * (t - j))
                V.scalar_tensor_tensor(y_out[:, j, :], banks(4), at("dq2", j), x1_in[:, j, :],
                                       ALU.mult, ALU.add).then_inc(S("y"), 1)

            def ffn_dve(t, j, more=True, first=False, y_first=False):
                if not first:
                    dve.wait_ge(S("gT_ps"), 4 * t)
                for n in range(4):
                    dve.wait_ge(S("g_magic"), 4 * t + n + 1)
                    V.tensor_scalar(hid_q[:, n * D:(n + 1) * D], hid[:, j, n * D:(n + 1) * D], -MAGIC, None,
                                    ALU.add).then_inc(S("g_q"), 1)
                if not first:
                    y_dve(t - 1, 1 - j, y_first)
                if more:
                    hid_max(t + 1, 1 - j, range(3))
                hidT_dve(t, j, 1)
                if more:
                    hid_max(t + 1, 1 - j, range(3, 4))
                    hid_scale(t + 1, 1 - j)
                hidT_dve(t, j, 3)

            def hidT_dve(t, j, n):
                dve.wait_ge(S("gT_ps"), 4 * t + n + 1)
                V.tensor_copy(hid_T[:, j, 8 * n:8 * n + 8, :], turned(7)).then_inc(S("gT_lo"), 1)

            hid_max(0, 0)
            hid_scale(0, 0)
            ffn_dve(0, 0, first=True)
            ffn_dve(1, 1, y_first=True)
            ffn_dve(2, 0, y_first=True)
            ffn_dve(3, 1)
            steps(dve, 4, 8, ffn_dve)
            ffn_dve(8, 0)
            ffn_dve(9, 1, False)
            y_dve(9, 1)

        @block.tensor
        def _(pe):
            mm = nc.tensor.matmul

            def product(acc, left, right, ready=None, halves="split", between={}):
                passes = ((0, 0), (0, 1), (1, 0)) if ready is None else ((0, 0), (1, 0), (0, 1))
                for kc in range(KC):
                    if kc in between:
                        between[kc]()
                    for i, (l, r) in enumerate(passes):
                        if ready is not None and i != 1:
                            pe.wait_ge(S(halves + ("_lo" if r else "_hi")), ready + kc + 1)
                        for n in range(2):
                            last = mm(acc[:, n * BANK:(n + 1) * BANK], left(l, kc),
                                      right(kc, r)[:, n * BANK:(n + 1) * BANK],
                                      start=(kc == 0 and i == 0), stop=(kc == KC - 1 and i == 2))
                return last

            def turn(bank, pieces, n=8):
                for k in range(n):
                    last = nc.tensor.transpose(turned(bank)[:, k, :], pieces(k), ident[:, :])
                return last

            def total(count, src, n):
                mm(ps[:, NORM_AT[count]:NORM_AT[count] + n], ones[:, :], src, start=True, stop=True)\
                    .then_inc(S("norm_ps"), 1)

            def xT_pe(t, j):
                wait(pe, "xT_hi", t)
                wait(pe, "xT_lo", t)
                pe.wait_ge(S("ln_hi"), t + 1)
                turn(2, lambda k: HL[:, j, 0, k * P:(k + 1) * P]).then_inc(S("xT_ps"), 1)
                pe.wait_ge(S("ln_lo"), t + 1)
                turn(3, lambda k: HL[:, j, 1, k * P:(k + 1) * P]).then_inc(S("xT_ps"), 1)

            def of_x(t):
                return lambda l, kc: XH[:, l, kc, tile_of(t)]

            def of(w):
                return lambda kc, r: w[:, kc, r, :]

            def kv_sum(t, j, first=False, last_rows=P):
                pe.wait_ge(S("k_lo"), t + 1)
                pe.wait_ge(S("v_lo"), t + 1)
                for p in range(KC):
                    c = slice(P * p, P * p + P)
                    for n, (a, b) in enumerate(((2, 0), (2, 1), (3, 0))):
                        last = mm(ps[:, 6 * BANK + P * p:6 * BANK + P * p + P], kv[0:last_rows, j, a, c],
                                  kv[0:last_rows, j, b, c], start=(first and n == 0 and p % 4 == 0),
                                  stop=(last_rows != P and n == 2), skip_group_check=True)
                last.then_inc(S("kv_ps"), 1)

            def k_pe(t, ready=None, between={}):
                wait(pe, "k_t", t)
                pe.wait_ge(S("xT_hi"), t + 1)
                pe.wait_ge(S("xT_lo"), t + 1)
                product(banks(0), of_x(t), of(Wk_s), ready, between=between).then_inc(S("k_ps"), 1)

            def v_pe(t, ready=None):
                wait(pe, "v_t", t)
                product(banks(4), of_x(t), of(Wv_s), ready).then_inc(S("v_ps"), 1)

            def kv_pe(t, j):
                k_pe(t)
                kv_sum(t - 1, 1 - j)
                xT_pe(t + 1, 1 - j)
                v_pe(t)

            def Wv_total():
                pe.wait_ge(S("sq"), 2)
                total(2, col("sq1"), 1)

            pe.wait_ge(S("ident"), 1)
            xT_pe(0, 0)
            pe.wait_ge(S("ones"), 1)
            pe.wait_ge(S("sq"), 1)
            total(1, col("sq0"), 1)
            k_pe(0, ready=0, between={4: lambda: xT_pe(1, 1)})
            k_pe(1, between={3: Wv_total})
            v_pe(0, ready=8)
            xT_pe(2, 0)
            v_pe(1)
            kv_sum(0, 0, first=True)
            kv_pe(2, 0)
            kv_pe(3, 1)
            pe.wait_ge(S("sq"), 4)
            pe.wait_ge(S("xT_hi"), 5)
            total(3, col("sq_q"), 2)
            k_pe(4)
            kv_sum(3, 1)
            pe.wait_ge(S("norm"), 3)
            xT_pe(5, 1)
            v_pe(4)
            kv_pe(5, 1)
            steps(pe, 6, 8, lambda t, j: kv_pe(t, j))
            kv_pe(8, 0)
            k_pe(9)
            kv_sum(8, 0)
            pe.wait_ge(S("sq"), 5)
            pe.wait_ge(S("xT_hi"), NT)
            total(4, col("sq5"), 5)
            v_pe(9)

            def q_pe(m, j, ready=None):
                wait(pe, "q_t", m - 1)
                mc = bass.ds(m * P, P)
                for kc in range(KC):
                    if ready is not None:
                        pe.wait_ge(S("split_lo"), ready + kc + 1)
                    for l, rs in ((0, (0, 1)), (1, (0,))):
                        for r in rs:
                            for a in range(0, N, BANK):
                                b = min(a + BANK, N)
                                last = mm(ps[:, 3 * j * BANK + a:3 * j * BANK + b], Wq_s[:, kc, l, mc],
                                          XH[:, r, kc, a:b], start=(kc == 0 and l == 0 and r == 0),
                                          stop=(kc == KC - 1 and l == 1))
                last.then_inc(S("q_ps"), 1)

            def m_pe(p, bank):
                for n in range(2):
                    last = mm(ps[:, (bank + n) * BANK:(bank + n + 1) * BANK], kvT[:, p * P:(p + 1) * P],
                              Wo_raw[:, p, n * BANK:(n + 1) * BANK], start=True, stop=True)
                last.then_inc(S("m_ps"), 1)

            def qm_pe(m, j):
                q_pe(m, j)
                pe.wait_ge(S("m_lo"), m - 3)
                m_pe(m - 3, 6)

            pe.wait_ge(S("k_t"), NT)
            pe.wait_ge(S("norm"), 4)
            q_pe(0, 0, ready=KC * WQ)
            pe.wait_ge(S("v_t"), NT)
            kv_sum(9, 1, last_rows=N - (NT - 1) * P)
            q_pe(1, 1)
            q_pe(2, 0)
            pe.wait_ge(S("kv_sq"), 1)
            total(5, col("kv_sq"), 1)
            q_pe(3, 1)
            pe.wait_ge(S("wo_in"), 16)
            pe.wait_ge(S("norm"), 5)
            m_pe(0, 6)
            for m in range(4, 8):
                qm_pe(m, m % 2)
            pe.wait_ge(S("q_t"), 8)
            for p in range(5, KC):
                if M_BANK[p] == 6:
                    pe.wait_ge(S("m_lo"), 5)
                m_pe(p, M_BANK[p])

            pe.wait_ge(S("q_lo"), 8)
            pe.wait_ge(S("pad0"), 1)

            def u_pe(t, j, ready=None):
                wait(pe, "u_t", t - 1)
                product(banks(4 * j), lambda l, p: qT[:, l, p, tile_of(t)], of(M_s), ready, "m")\
                    .then_inc(S("u_ps"), 1)

            u_pe(0, 0, ready=0)
            u_pe(1, 1)
            steps(pe, 2, NT, u_pe)

            done = pe.alloc_register("done")
            pe.reg_mov(done, 0)
            parts = [(a, min(a + BANK, N)) for a in range(0, N, BANK)]

            def aT_pe(t):
                pe.wait_ge(S("a_row"), t + 1)
                wait(pe, "aT_lo", t)
                turn(3, lambda k: a_row[:, k * P:(k + 1) * P]).then_inc(S("aT_ps"), 1)

            def aT_rest_pe(t):
                pe.wait_ge(S("aT_hi"), t + 1)
                turn(3, lambda k: a_row[:, (8 + k) * P:(9 + k) * P], NT - 8).then_inc(S("aT_ps"), 1)

            def hots(start=False):
                n = pe.snap(done)
                for j in range(QUAD):
                    pe.wait_ge(S("hot_src"), n + (j + 1))
                    pe.wait_ge(S("hot_dst"), n + (j + 1))
                    for a, z in parts:
                        one = mm(ps[:, a:z], hot_dst[:, j, :], hot_src[:, j, a:z], start=(start and j == 0), stop=False,
                                 skip_group_check=True)
                    one.then_inc(S("hot_free"), 1)
                pe.reg_add(done, done, QUAD)

            def mean_total():
                pe.wait_ge(S("sq"), 6)
                pe.wait_ge(S("z0_lo"), 1)
                mm(ps[:, MEAN_AT:MEAN_AT + 2], ones[:, :], col("w_sum"), start=True, stop=True).then_inc(S("mean_ps"), 1)

            def count_pe(t, j, more={}):
                first = pe.value_load(bnd[0:1, 0, bass.ds(t, 1)], min_val=0, max_val=EC - 1)
                last = pe.value_load(bnd[0:1, 1, bass.ds(t, 1)], min_val=QUAD + 1, max_val=EC + QUAD)
                wait(pe, "a_row", t)
                hots(start=True)
                with pe.Fori(first + QUAD, last, QUAD):
                    hots()
                for a, z in parts:
                    one = mm(ps[:, a:a + 2], zero[:, :], iota[:, 0:2], start=False, stop=True, skip_group_check=True)
                one.then_inc(S("a_ps"), 1)
                if isinstance(t, int) and t == 0:
                    pe.wait_ge(S("split_lo"), 32)
                    pe.wait_ge(S("u_t"), NT)
                wait(pe, "z0_lo", t - 1)
                product(banks(4 + 2 * j), of_x(t), of(weight(S0)),
                        between={3: lambda: aT_pe(t), 5: lambda: aT_rest_pe(t), **more}).then_inc(S("z0_ps"), 1)

            pe.wait_ge(S("zero"), 1)
            pe.wait_ge(S("iota"), 1)
            pe.wait_ge(S("bounds"), 2)
            pe.wait_ge(S("u_t"), NT - 1)
            pe.wait_ge(S("pad0"), 2)
            count_pe(0, 0)
            count_pe(1, 1, {6: mean_total})
            steps(pe, 2, NT, count_pe)

            def edge_sum(t, name, bank=0):
                for s in range(NT):
                    for r in range(2):
                        for n in range(2):
                            last = mm(banks(bank + n, 1), ATv[:, s, tile_of(t)],
                                      Z[:, r, s, n * BANK:(n + 1) * BANK], start=(s == 0 and r == 0),
                                      stop=(s == NT - 1 and r == 1))
                last.then_inc(S(name), 1)

            def hT_pe(t, j):
                wait(pe, "hT_hi", t)
                wait(pe, "hT_lo", t)
                pe.wait_ge(S("h_hi"), t + 1)
                turn(6, lambda k: HL[:, j, 0, k * P:(k + 1) * P]).then_inc(S("hT_ps"), 1)
                pe.wait_ge(S("h_lo"), t + 1)
                turn(7, lambda k: HL[:, j, 1, k * P:(k + 1) * P]).then_inc(S("hT_ps"), 1)

            def s0_pe(t):
                wait(pe, "h_t2", t)
                product(banks(2), of_x(t), of(weight(S1))).then_inc(S("s0_ps"), 1)

            def h_pe(t, j, first=False):
                if not first:
                    wait(pe, "h_t1", t)
                edge_sum(t, "g0_ps")
                hT_pe(t - 1, 1 - j)
                s0_pe(t)

            pe.wait_ge(S("split_lo"), 40)
            pe.wait_ge(S("aT_hi"), NT)
            pe.wait_ge(S("aT_lo"), NT)
            s0_pe(0)
            pe.wait_ge(S("z0_hi"), NT)
            pe.wait_ge(S("z0_lo"), NT)
            edge_sum(0, "g0_ps", 4)
            h_pe(1, 1, first=True)
            steps(pe, 2, NT, h_pe)

            def z1_pe(t, j, between={}):
                wait(pe, "z1_lo", t - 1)
                product(banks(4 * j), of_x(t), of(weight(S0)), between=between).then_inc(S("z1_ps"), 1)

            def h_total():
                pe.wait_ge(S("sq"), 7)
                total(6, col("sq_h"), 1)

            pe.wait_ge(S("split_lo"), 48)
            pe.wait_ge(S("hT_hi"), NT - 1)
            pe.wait_ge(S("hT_lo"), NT - 1)
            pe.wait_ge(S("h_t1"), NT)
            z1_pe(0, 0)
            hT_pe(NT - 1, 1)
            pe.wait_ge(S("hT_hi"), NT)
            pe.wait_ge(S("hT_lo"), NT)
            pe.wait_ge(S("h_sq"), NT)
            z1_pe(1, 1, {2: h_total})
            steps(pe, 2, NT, z1_pe)

            def x2T_pe(t, j):
                wait(pe, "x2T", t)
                pe.wait_ge(S("r"), t + 1)
                turn(6, lambda k: r_rows[:, j, k * P:(k + 1) * P]).then_inc(S("x2T_ps"), 1)

            def s1_pe(t, between={}):
                wait(pe, "x1", t)
                product(banks(2), of_x(t), of(weight(S1)), between=between).then_inc(S("s1_ps"), 1)

            def x1_pe(t, j, first=False):
                if not first:
                    wait(pe, "x1_t1", t)
                edge_sum(t, "g1_ps")
                s1_pe(t, {4: lambda: x2T_pe(t - 1, 1 - j)})

            pe.wait_ge(S("split_lo"), 56)
            pe.wait_ge(S("h_t2"), NT)
            s1_pe(0)
            pe.wait_ge(S("z1_hi"), NT)
            pe.wait_ge(S("z1_lo"), NT)
            edge_sum(0, "g1_ps", 4)
            x1_pe(1, 1, first=True)
            steps(pe, 2, NT, x1_pe)

            def f1_pe(t, j, between={}):
                pe.wait_ge(S("x2_tile"), t + 1)
                for n in range(8):
                    if n in between:
                        between[n]()
                    if n % 2 == 0:
                        wait(pe, "gelu", 8 * t + n - 2)
                        alone(pe)
                    for kc in range(KC):
                        last = mm(banks(n % 4, 1), x2_tile[:, j, kc, :], w1q[:, kc, n * BANK:(n + 1) * BANK],
                                  start=(kc == 0), stop=(kc == KC - 1))
                    last.then_inc(S("f1_ps"), 1)

            def gT_pe(t, j, n):
                wait(pe, "gT_lo" if n % 2 else "gT_hi", 2 * t + n // 2)
                pe.wait_ge(S("g_q"), 4 * t + n + 1)
                turn(6 + n % 2, lambda k: hid_q[:, (8 * n + k) * P:(8 * n + k + 1) * P]).then_inc(S("gT_ps"), 1)

            def f2_pe(t, j, n):
                pe.wait_ge(S("gT_lo" if n % 2 else "gT_hi"), 2 * t + n // 2 + 1)
                alone(pe)
                for kc in range(8 * n, 8 * n + 8):
                    for h in range(2):
                        last = mm(banks(4 + h, 1), hid_T[:, j, kc, :], w2q[:, kc, h * BANK:(h + 1) * BANK],
                                  start=(kc == 0), stop=(kc == HC - 1))
                return last

            def out_pe(t, j):
                gT_pe(t, j, 1)
                wait(pe, "y", t)
                f2_pe(t, j, 0)
                gT_pe(t, j, 2)
                f2_pe(t, j, 1)
                gT_pe(t, j, 3)
                f2_pe(t, j, 2)
                f2_pe(t, j, 3).then_inc(S("f2_ps"), 1)

            def ffn_pe(t, j):
                f1_pe(t + 1, 1 - j, {7: lambda: gT_pe(t, j, 0)})
                out_pe(t, j)

            pe.wait_ge(S("w1q_in"), 16)
            pe.wait_ge(S("x1_t1"), NT)
            f1_pe(0, 0, {2: lambda: pe.wait_ge(S("x1"), NT)})
            x2T_pe(NT - 1, 1)

            def first_turn():
                pe.wait_ge(S("x2T"), NT)
                gT_pe(0, 0, 0)

            f1_pe(1, 1, {7: first_turn})
            pe.wait_ge(S("w2q_in"), 16)
            out_pe(0, 0)
            ffn_pe(1, 1)
            steps(pe, 2, 8, ffn_pe)
            ffn_pe(8, 0)
            gT_pe(9, 1, 0)
            out_pe(9, 1)


def kernel(**inputs):
    import numpy as np
    import concourse.bacc as bacc
    from concourse.bass_utils import run_bass_kernel_spmd

    a = {k: np.asarray(v) for k, v in inputs.items()}
    x = np.zeros((NP_, D), np.float32)
    x[:N] = a["x"]
    src = np.full(ECP * P, 2 * NP_, np.int32)
    src[:NE] = a["src"]
    dst = np.full(ECP * P, NP_ - 1, np.int32)
    dst[:NE] = a["dst"]
    dst_rows = np.full((2 * P, P), 4 * NP_, np.int32)
    dst_rows[:EC] = dst.reshape(ECP, P)[:EC]
    arrays = dict(
        x=x, src_cols=src.reshape(ECP, P).T, dst_cols=dst.reshape(ECP, P).T, dst_rows=dst_rows,
        Wself0=a["L0_gnn_W_self0"], Wneigh0=a["L0_gnn_W_neigh0"], b0=a["L0_gnn_b0"],
        Wself1=a["L0_gnn_W_self1"], Wneigh1=a["L0_gnn_W_neigh1"], b1=a["L0_gnn_b1"],
        Wq=a["L0_mix_Wq"], bq_cols=a["L0_mix_bq"].reshape(KC, P).T, Wk=a["L0_mix_Wk"], bk=a["L0_mix_bk"],
        Wv=a["L0_mix_Wv"], bv=a["L0_mix_bv"], Wo=a["L0_mix_Wo"], bo=a["L0_mix_bo"],
        w1t=a["L0_ffn_w1"].T, w2t=a["L0_ffn_w2"].T)
    arrays["w_all"] = np.concatenate([arrays[k] for k in ("Wq", "Wo", "Wneigh0", "Wself0", "Wneigh1", "Wself1")])
    arrays = {k: np.ascontiguousarray(v) for k, v in arrays.items()}
    nc = bacc.Bacc("TRN2", target_bir_lowering=False, num_devices=1, dynamic_dma_scratch_size=1024)
    args = {k: nc.dram_tensor(f"in_{k}", v.shape, mybir.dt.from_np(v.dtype), kind="ExternalInput").ap()
            for k, v in arrays.items()}
    out = nc.dram_tensor("out", (NP_, D), F32, kind="ExternalOutput").ap()
    gps_kernel(nc, **args, out=out)
    r = run_bass_kernel_spmd(nc, [{f"in_{k}": v for k, v in arrays.items()}], core_ids=[0])
    return r.results[0]["out"][:N]
```
